# Optimizing a Trainium2 kernel written in Bass

```python
import numpy as np
import jax
import jax.numpy as jnp

def _softmax(x, axis=-1):
    return jax.nn.softmax(x, axis=axis)

def _gelu(x):
    return jax.nn.gelu(x, approximate=True)

def _silu(x):
    return jax.nn.silu(x)

def _sigmoid(x):
    return jax.nn.sigmoid(x)

def _layernorm(x, axis=-1, eps=1e-05):
    m = jnp.mean(x, axis=axis, keepdims=True)
    v = jnp.var(x, axis=axis, keepdims=True)
    return (x - m) / jnp.sqrt(v + eps)

def _scatter_add(tgt, idx, src, axis=0):
    return tgt.at[idx].add(src)

def _segment_sum(src, seg, n):
    return jax.ops.segment_sum(src, seg, n)
kernel_name = 'mk_adaln_ffn_d1_seqx_r2_178a76'

def setup_inputs(seed: int=0):
    np.random.seed(seed)
    _w = jnp.asarray

    def _rec_inputs():
        import jax
        import jax.numpy as jnp
        _rk = jax.random.key(seed)
        x = -0.000125 + 0.9999 * jax.random.normal(jax.random.fold_in(_rk, 1), (2, 2048, 512), jnp.float32)
        _lenS = 2048 - jax.random.randint(jax.random.fold_in(_rk, 7), (2,), 0, max(1, 2048 // 4) + 1, jnp.int32)
        _lenS2 = 2048 - jax.random.randint(jax.random.fold_in(_rk, 8), (2,), 0, max(1, 2048 // 4) + 1, jnp.int32)
        cond_1024 = 0.00513981 + 1.0024 * jax.random.normal(jax.random.fold_in(_rk, 11), (2, 512), jnp.float32)
        return (x, cond_1024)
    x, cond_1024 = _rec_inputs()

    def _L0_cond_setup():
        import jax, jax.numpy as jnp
        import numpy as np
        IN_FEATURES = 512
        OUT_FEATURES = 512
        BATCH = 32
        SEQ = 512
        EPS = 1e-08
        key = jax.random.key(seed)
        k1, k2, k3 = jax.random.split(key, 3)
        Efou = jax.random.normal(k1, (BATCH, SEQ, IN_FEATURES), dtype=jnp.float32)
        y = jax.random.normal(k2, (BATCH, IN_FEATURES), dtype=jnp.float32)
        weight = jax.random.normal(k3, (IN_FEATURES, OUT_FEATURES), dtype=jnp.float32)
        return {'Efou': Efou, 'y': y, 'weight': weight}
    _L0_cond_all = _L0_cond_setup()
    _L0_cond_in = {k: v for k, v in _L0_cond_all.items() if k in ('weight',)}
    del _L0_cond_all

    def _L0_ffn_setup():
        import jax, jax.numpy as jnp
        import numpy as np
        D_MODEL = 512
        HIDDEN = 2048
        N_ROUTING = 2
        key = jax.random.key(seed)
        ks = jax.random.split(key, 10)
        s = 0.02
        x = jax.random.normal(ks[0], (4, 2048, D_MODEL), dtype=jnp.float32)
        gate_w = jax.random.normal(ks[1], (N_ROUTING, D_MODEL), dtype=jnp.float32) * s
        w1 = jax.random.normal(ks[2], (N_ROUTING, D_MODEL, HIDDEN), dtype=jnp.float32) * s
        b1 = jax.random.normal(ks[3], (N_ROUTING, HIDDEN), dtype=jnp.float32) * s
        w2 = jax.random.normal(ks[4], (N_ROUTING, HIDDEN, D_MODEL), dtype=jnp.float32) * s
        b2 = jax.random.normal(ks[5], (N_ROUTING, D_MODEL), dtype=jnp.float32) * s
        sw1 = jax.random.normal(ks[6], (D_MODEL, HIDDEN), dtype=jnp.float32) * s
        sb1 = jax.random.normal(ks[7], (HIDDEN,), dtype=jnp.float32) * s
        sw2 = jax.random.normal(ks[8], (HIDDEN, D_MODEL), dtype=jnp.float32) * s
        sb2 = jax.random.normal(ks[9], (D_MODEL,), dtype=jnp.float32) * s
        return {'x': x, 'gate_w': gate_w, 'w1': w1, 'b1': b1, 'w2': w2, 'b2': b2, 'sw1': sw1, 'sb1': sb1, 'sw2': sw2, 'sb2': sb2}
    _L0_ffn_all = _L0_ffn_setup()
    _L0_ffn_in = {k: v for k, v in _L0_ffn_all.items() if k in ('gate_w', 'w1', 'b1', 'w2', 'b2', 'sw1', 'sb1', 'sw2', 'sb2')}
    del _L0_ffn_all
    return {'x': x, 'cond_1024': cond_1024, 'L0_cond_weight': _L0_cond_in['weight'], 'L0_ffn_gate_w': _L0_ffn_in['gate_w'], 'L0_ffn_w1': _L0_ffn_in['w1'], 'L0_ffn_b1': _L0_ffn_in['b1'], 'L0_ffn_w2': _L0_ffn_in['w2'], 'L0_ffn_b2': _L0_ffn_in['b2'], 'L0_ffn_sw1': _L0_ffn_in['sw1'], 'L0_ffn_sb1': _L0_ffn_in['sb1'], 'L0_ffn_sw2': _L0_ffn_in['sw2'], 'L0_ffn_sb2': _L0_ffn_in['sb2']}

def reference(x, cond_1024, L0_cond_weight, L0_ffn_gate_w, L0_ffn_w1, L0_ffn_b1, L0_ffn_w2, L0_ffn_b2, L0_ffn_sw1, L0_ffn_sb1, L0_ffn_sw2, L0_ffn_sb2):
    import jax
    import jax.numpy as jnp

    def _L0_cond_ref(Efou, y, weight):
        import jax, jax.numpy as jnp
        import numpy as np
        IN_FEATURES = 512
        OUT_FEATURES = 512
        BATCH = 32
        SEQ = 512
        EPS = 1e-08
        scale = 1.0 / np.sqrt(np.float32(weight.shape[0]))
        ys = y * scale
        d = jax.lax.rsqrt(jnp.einsum('bi,io->bo', ys * ys, weight * weight) + EPS)
        out = jnp.einsum('bsi,io->bso', Efou * ys[:, None, :], weight) * d[:, None, :]
        return out

    def _L0_ffn_ref(x, gate_w, w1, b1, w2, b2, sw1, sb1, sw2, sb2):
        import jax, jax.numpy as jnp
        import numpy as np
        D_MODEL = 512
        HIDDEN = 2048
        N_ROUTING = 2
        B, S, D = x.shape
        xf = x.reshape(-1, D)
        gate_scores = xf @ gate_w.T
        gate_probs = jax.nn.softmax(gate_scores, axis=-1)
        top1 = jnp.argmax(gate_probs, axis=-1)
        one_hot = jax.nn.one_hot(top1, N_ROUTING, dtype=xf.dtype)
        masked = xf[None, :, :] * one_hot.T[:, :, None]
        h = jax.nn.relu(jnp.einsum('end,edh->enh', masked, w1) + b1[:, None, :])
        expert_out = jnp.einsum('enh,ehd->end', h, w2) + b2[:, None, :]
        routing_output = expert_out.sum(axis=0)
        shared = jax.nn.relu(xf @ sw1 + sb1) @ sw2 + sb2
        return (routing_output + shared).reshape(B, S, D)
    x = x + _L0_ffn_ref(_L0_cond_ref(x, cond_1024, L0_cond_weight), L0_ffn_gate_w, L0_ffn_w1, L0_ffn_b1, L0_ffn_w2, L0_ffn_b2, L0_ffn_sw1, L0_ffn_sb1, L0_ffn_sw2, L0_ffn_sb2)
    return x

_drawn_inputs = setup_inputs


def setup_inputs(seed=0):
    import zlib

    import numpy as np

    out = dict(_drawn_inputs(seed))
    spreads = {}
    factors = {'L0_ffn_b1': 3.619, 'L0_ffn_sb1': 4.866, 'L0_ffn_sb2': 3.102}
    for name, (base, spread) in spreads.items():
        noise = np.random.default_rng([zlib.crc32(name.encode()), seed]).standard_normal(out[name].shape)
        drawn = base * np.exp(spread * noise) if base else spread * noise
        out[name] = jnp.asarray(drawn.astype(out[name].dtype))
    for name, factor in factors.items():
        out[name] = (out[name] * factor).astype(out[name].dtype)
    return out
```

```python
from contextlib import ExitStack

import concourse.bass as bass
from concourse import mybir

F32 = mybir.dt.float32
F32R = mybir.dt.float32r
I32 = mybir.dt.int32
ALU = mybir.AluOpType
ACT = mybir.ActivationFunctionType
AX = mybir.AxisListType

P = 128
N = 4096
D = 512
H = 2048
KD = D // P
HC = H // P
T = 512
M = T // P
NT = N // P
RING = 4
ROUNDS = NT // RING
BATCHES = 2
SHARED = N // T
EXPERT = N // T + 1
SLOTS = SHARED + EXPERT
COLS = (EXPERT + 1) * M
IDW = 16
PAD = N
EPS = 1e-8
DMA = 16


def wait(eng, sem, value):
    if isinstance(value, int) and value <= 0:
        return
    eng.wait_ge(sem, value)


def wait_apart(eng, sem, value, held):
    if not isinstance(value, int):
        value = eng.snap(value)
        eng.wait_ge(held, 1)
    eng.wait_ge(sem, value)


def block_of(ap, i):
    return ap[i] if isinstance(i, int) else ap[bass.ds(i, 1)].rearrange("a p n -> (a p) n")


def columns(ap, i, n=1):
    return ap[:, i:i + n] if isinstance(i, int) else ap[:, bass.ds(i, n)]


def chunk(ap, j):
    return columns(ap, j).rearrange("p a n -> p (a n)")


def token_rows(ap, n0, n):
    return ap[n0:n0 + n, :] if isinstance(n0, int) else ap[bass.ds(n0, n), :]


def slot_rows(ap, s):
    return token_rows(ap, s * T, T).rearrange("(m p) n -> p m n", p=P)


def build(nc, x_rows, x_cols, cond, w_cond, w_pack, b1_pack, b2_rows, gate, out):
    xf_dram = nc.dram_tensor("xf_scratch", (N, D), F32).ap()
    part_dram = nc.dram_tensor("partial_scratch", (N, D), F32).ap()
    table_dram = nc.dram_tensor("token_table", (COLS * P, IDW), I32).ap()

    with ExitStack() as ctx:
        def sb(name, shape, dt=F32):
            return ctx.enter_context(nc.sbuf_tensor(name, shape, dt))

        def pb(name):
            return ctx.enter_context(nc.psum_tensor(name, [P, 512], F32))

        def sem(name):
            return ctx.enter_context(nc.semaphore(name))

        w_hi = sb("w_hi", [P, HC, 1024], F32R)
        w_lo = sb("w_lo", [P, HC, 1024], F32R)
        stage = sb("stage", [P, 2, 1024])
        rows = sb("rows", [P, M, D])
        res = sb("res", [P, M, D])
        x_hi = sb("x_hi", [P, KD, T], F32R)
        x_lo = sb("x_lo", [P, KD, T], F32R)
        hf = sb("hf", [P, 2, T])
        h_hi = sb("h_hi", [P, 2, T], F32R)
        h_lo = sb("h_lo", [P, 2, T], F32R)
        scratch = sb("scratch", [P, 4, D])
        junk = sb("junk", [P, D])
        bias = sb("bias", [P, 3, D])
        gate_w = sb("gate_w", [P, 2, D])
        ident = sb("ident", [P, P])
        ones = sb("ones", [P, P])
        before = sb("before", [P, P])
        b1 = sb("b1", [P, 3, HC])
        b1_relu = sb("b1_relu", [P, 3, HC])
        cnd = sb("cnd", [P, KD, BATCHES])
        ys = sb("ys", [P, KD, BATCHES])
        ys2 = sb("ys2", [P, KD, BATCHES])
        dcol = sb("dcol", [P, 4, KD * BATCHES])
        score4 = sb("score4", [P, 2, RING])
        score = sb("score", [P, ROUNDS, 2, RING])
        soft = sb("soft", [P, 8, NT])
        pick0 = sb("pick0", [P, NT])
        rank = sb("rank", [P, 2, NT])
        scan = sb("scan", [P, 2, NT])
        place = sb("place", [P, 4, NT])
        order = sb("order", [P, NT])
        steps = sb("steps", [P, 8])
        over = sb("over", [P, 8])
        t0_f = sb("t0_f", [P, 2])
        t0_i = sb("t0_i", [P, 1], I32)
        pos = sb("pos", [P, NT], I32)
        tab = sb("tab", [P, COLS], I32)
        tab_in = sb("tab_in", [P, COLS], I32)
        idx_rows = sb("idx_rows", [P, M], I32)
        idx_res = sb("idx_res", [P, M], I32)
        idx_out = sb("idx_out", [P, M], I32)

        w_raw = rows
        ring = res
        xo = hf
        acc = scratch[:, 0:2, :]
        aux = scratch[:, 2:4, :]
        d1_row = bias[:, 1, :]
        ids = gate_w[:, :, :].rearrange("p e n -> p (e n)")[:, 0:NT * IDW].bitcast(I32)
        pads = junk[:, 0:COLS * IDW // 2].bitcast(I32)

        y_ps = [pb(f"y_ps{m}") for m in range(M)]
        h_ps = [pb(f"h_ps{i}") for i in range(2)]
        t_ps = [pb(f"t_ps{i}") for i in range(2)]

        const_in = sem("const_in")
        w_raw_in = sem("w_raw_in")
        ring_in = [sem(f"ring_in{i}") for i in range(RING)]
        stage_in = [sem(f"stage_in{i}") for i in range(2)]
        rows_in = sem("rows_in")
        res_in = sem("res_in")
        rows_gathered = sem("rows_gathered")
        res_gathered = sem("res_gathered")
        aux_in = sem("aux_in")
        consts_made = sem("consts_made")
        sq_ready = sem("sq_ready")
        v_ready = sem("v_ready")
        d_step = sem("d_step")
        root_ready = sem("root_ready")
        diag_ready = sem("diag_ready")
        d_ready = sem("d_ready")
        d1_row_ready = sem("d1_row_ready")
        wc_step = sem("wc_step")
        wc0_ready = sem("wc0_ready")
        wc1_step = sem("wc1_step")
        tile_hi = sem("tile_hi")
        tile_lo = sem("tile_lo")
        tile_mm = sem("tile_mm")
        xf_ready = sem("xf_ready")
        xf_out = [sem(f"xf_out{i}") for i in range(2)]
        gate_half = sem("gate_half")
        gate_done = sem("gate_done")
        score_kept = sem("score_kept")
        route = sem("route")
        soft_in = sem("soft_in")
        soft_exp = sem("soft_exp")
        pick_ready = sem("pick_ready")
        rank_ps = sem("rank_ps")
        t0_ready = sem("t0_ready")
        pos_ready = sem("pos_ready")
        pads_made = sem("pads_made")
        pads_out = sem("pads_out")
        ids_made = sem("ids_made")
        ids_out = sem("ids_out")
        tab_dma = sem("tab_dma")
        tab_ready = sem("tab_ready")
        idx_made = sem("idx_made")
        w_hi_made = sem("w_hi_made")
        w_ready = sem("w_ready")
        xt_ps = sem("xt_ps")
        xt_hi = sem("xt_hi")
        xt_lo = sem("xt_lo")
        h_mm = sem("h_mm")
        hf_ready = sem("hf_ready")
        hh_ready = sem("hh_ready")
        h_ready = sem("h_ready")
        y_mm = sem("y_mm")
        res_biased = sem("res_biased")
        out_ready = sem("out_ready")
        part_out = sem("part_out")
        scattered = sem("scattered")
        acc_step = sem("acc_step")
        bias_ps = sem("bias_ps")
        bias_step = sem("bias_step")

        def read_t0(eng):
            return eng.value_load(t0_i[0:1, 0:1], min_val=1, max_val=SHARED)

        block = ctx.enter_context(nc.Block())

        @block.sync
        def _(sp):
            sp.dma_start(w_raw[:], w_cond).then_inc(w_raw_in, DMA)
            sp.dma_start(cnd[:], cond).then_inc(const_in, DMA)
            sp.dma_start(gate_w[:], gate.partition_broadcast(P)).then_inc(const_in, DMA)
            for i in range(RING):
                sp.dma_start(ring[:, i, :], x_cols[i]).then_inc(ring_in[i], DMA)
            sp.dma_start(b1[:], b1_pack).then_inc(const_in, DMA)
            sp.dma_start(bias[:, 0, :], b2_rows[0].partition_broadcast(P)).then_inc(const_in, DMA)
            for i in range(2):
                sp.dma_start(stage[:, i, :], w_pack[i]).then_inc(stage_in[i], DMA)

            def weight_chunks(u):
                for i in range(2):
                    sp.wait_ge(w_ready, 2 * u + i - 1)
                    sp.dma_start(stage[:, i, :], block_of(w_pack, 2 * u + i)).then_inc(stage_in[i], DMA)

            def tiles_round(t, more):
                for i in range(RING):
                    c = t * RING + i
                    sp.wait_ge(xf_ready, c + 1)
                    sp.dma_start(token_rows(xf_dram, c * P, P), xo[:, i % 2, :]).then_inc(xf_out[i % 2], DMA)
                    if more:
                        sp.wait_ge(tile_lo, c + 1)
                        sp.dma_start(ring[:, i, :], block_of(x_cols, c + RING)).then_inc(ring_in[i], DMA)

            with sp.Fori(0, 4) as t:
                tiles_round(t, True)
                weight_chunks(t + 1)
            for i in range(2):
                sp.wait_ge(xf_out[i], 2 * DMA)
            sp.wait_ge(wc1_step, KD + 3)
            sp.dma_start(rows[:], slot_rows(xf_dram, 0)).then_inc(rows_in, DMA)
            with sp.Fori(4, ROUNDS - 1) as t:
                tiles_round(t, True)
            tiles_round(ROUNDS - 1, False)

            sp.wait_ge(tile_lo, NT)
            sp.dma_start(res[:], slot_rows(x_rows, 0)).then_inc(res_in, DMA)

            w2_pair = w_pack.rearrange("(f j) p n -> j p f n", f=3)[:, :, 1:3, D:2 * D]

            def aux_load(j):
                sp.wait_ge(acc_step, 2 + 2 * j)
                src = w2_pair[j] if isinstance(j, int) else w2_pair[bass.ds(j, 1)].rearrange("a p f n -> (a p) f n")
                sp.dma_start(aux, src).then_inc(aux_in, DMA)

            aux_load(0)
            for u in range(5, HC // 2 + 1):
                weight_chunks(u)
            for i in range(2):
                sp.wait_ge(xf_out[i], DMA * NT // 2)

            def slot_loads(s, more):
                if more:
                    sp.wait_ge(xt_ps, KD * (s + 1))
                    sp.dma_start(rows[:], slot_rows(xf_dram, s + 1)).then_inc(rows_in, DMA)
                aux_load(2 * s + 1)
                if more:
                    aux_load(2 * s + 2)
                else:
                    sp.wait_ge(acc_step, 2 + 2 * HC)
                    for e in range(2):
                        sp.dma_start(aux[:, e, :], b2_rows[1 + e].partition_broadcast(P)).then_inc(const_in, DMA)
                for m in range(M):
                    sp.wait_ge(out_ready, M * s + m + 1)
                    sp.dma_start(token_rows(part_dram, (M * s + m) * P, P), res[:, m, :]).then_inc(part_out, DMA)
                if more:
                    sp.wait_ge(part_out, M * DMA * (s + 1))
                    sp.dma_start(res[:], slot_rows(x_rows, s + 1)).then_inc(res_in, DMA)

            with sp.Fori(0, SHARED - 1) as s:
                slot_loads(s, True)
            slot_loads(SHARED - 1, False)
            with sp.Fori(HC // 2 + 1, 3 * HC // 2) as u:
                weight_chunks(u)

        @block.gpsimd
        def _(pool):
            pool.memset(ident[:], 0.0).then_inc(pads_made, 1)
            pool.memset(ones[:], 1.0).then_inc(pads_made, 1)
            pool.memset(pads, PAD).then_inc(pads_made, 1)
            pool.wait_ge(pads_made, 3)
            pool.affine_select(out=ident[:], in_=ident[:], compare_op=ALU.not_equal, fill=1.0, base=0,
                               pattern=[[-1, P]], channel_multiplier=1).then_inc(consts_made, 1)
            pool.affine_select(out=before[:], in_=ones[:], compare_op=ALU.is_gt, fill=0.0, base=0,
                               pattern=[[1, P]], channel_multiplier=-1).then_inc(consts_made, 1)
            pool.iota(order[:], [[P, NT]], base=0, channel_multiplier=1,
                      allow_small_or_imprecise_dtypes=True).then_inc(consts_made, 1)
            pool.iota(steps[:], [[T, 8]], base=0, channel_multiplier=0,
                      allow_small_or_imprecise_dtypes=True).then_inc(consts_made, 1)
            half = COLS * IDW // 2
            table_p = table_dram.rearrange("(p c) w -> p (c w)", p=P)
            for i in range(2):
                pool.dma_start(table_p[:, i * half:(i + 1) * half], pads).then_inc(pads_out, DMA)

            pool.wait_ge(w_raw_in, DMA)
            pool.wait_ge(d1_row_ready, 1)
            pool.wait_ge(v_ready, 1)
            for k in range(KD):
                pool.tensor_scalar(scratch[:, k, :], w_raw[:, k, :], ys[:, k, 1:2], None, ALU.mult).then_inc(wc1_step, 1)
            pool.wait_ge(wc1_step, KD)
            pool.tensor_tensor(scratch[:], scratch[:], d1_row.unsqueeze(1).broadcast_to([P, KD, D]),
                               ALU.mult).then_inc(wc1_step, 1)
            pool.wait_ge(wc1_step, KD + 1)
            wc1 = w_hi[:, 8:12, 512:1024], w_lo[:, 8:12, 512:1024]
            pool.tensor_copy(wc1[0], scratch[:]).then_inc(wc1_step, 1)
            pool.wait_ge(wc1_step, KD + 2)
            pool.tensor_tensor(wc1[1], scratch[:], wc1[0].bitcast(F32), ALU.subtract).then_inc(wc1_step, 1)

            def split_chunk(i, ch, j):
                hi, lo = chunk(w_hi, j), chunk(w_lo, j)
                pool.tensor_copy(hi, stage[:, i, :]).then_inc(w_hi_made, 1)
                wait_apart(pool, w_hi_made, ch + 1, consts_made)
                pool.tensor_tensor(lo, stage[:, i, :], hi.bitcast(F32), ALU.subtract).then_inc(w_ready, 1)

            def first_chunks(u):
                for i in range(2):
                    wait_apart(pool, stage_in[i], DMA * (u + 1), consts_made)
                    split_chunk(i, 2 * u + i, 2 * u + i)

            with pool.Fori(0, HC // 4) as u:
                first_chunks(u)
            pool.wait_ge(tile_mm, NT)
            with pool.Fori(HC // 4, HC // 2) as u:
                first_chunks(u)

            pool.wait_ge(gate_done, NT)
            pool.iota(ids, [[P, NT], [0, IDW]], base=0, channel_multiplier=1).then_inc(ids_made, 1)
            pool.wait_ge(ids_made, 1)
            pool.wait_ge(pads_out, 2 * DMA)
            pool.wait_ge(pos_ready, 1)
            for c in range(NT):
                pool.indirect_dma_start(table_dram, bass.IndirectOffsetOnAxis(pos[:, c:c + 1], 0),
                                        ids[:, c * IDW:(c + 1) * IDW], None).then_inc(ids_out, DMA)
            pool.wait_ge(ids_out, NT * DMA)
            with nc.allow_non_contiguous_dma(reason="one number per 64-byte row"):
                pool.dma_start(tab[:], table_dram.rearrange("(c p) w -> p c w", p=P)[:, :, 0]).then_inc(tab_dma, DMA)
            pool.wait_ge(tab_dma, DMA)
            pool.tensor_scalar(tab_in[:], tab[:], N - 1, None, ALU.min).then_inc(tab_ready, 1)
            pool.wait_ge(tab_ready, 1)

            def numbers(dst, table, s, count):
                pool.tensor_copy(dst[:], columns(table, (s - SHARED) * M, M)).then_inc(idx_made, 1)
                pool.drain()

            def gather_rows(s, count):
                wait_apart(pool, xt_ps, KD * s, tab_ready)
                numbers(idx_rows, tab_in, s, count)
                for m in range(M):
                    pool.indirect_dma_start(rows[:, m, :], None, xf_dram,
                                            bass.IndirectOffsetOnAxis(idx_rows[:, m:m + 1], 0)).then_inc(rows_gathered, DMA)

            def gather_res(s, count):
                if isinstance(s, int):
                    pool.wait_ge(part_out, M * DMA * SHARED)
                else:
                    wait_apart(pool, scattered, M * DMA * (s - SHARED), tab_ready)
                numbers(idx_res, tab_in, s, count)
                for m in range(M):
                    pool.indirect_dma_start(res[:, m, :], None, part_dram,
                                            bass.IndirectOffsetOnAxis(idx_res[:, m:m + 1], 0)).then_inc(res_gathered, DMA)

            def scatter_out(s, count):
                wait_apart(pool, out_ready, M * (s + 1), tab_ready)
                numbers(idx_out, tab, s, count)
                for m in range(M):
                    pool.indirect_dma_start(out, bass.IndirectOffsetOnAxis(idx_out[:, m:m + 1], 0),
                                            res[:, m, :], None, bounds_check=N - 1,
                                            oob_is_err=False).then_inc(scattered, DMA)

            def next_chunks(ffn, last):
                def two(u):
                    for i in range(2):
                        wait_apart(pool, y_mm, last * HC + 2 * u + i + 1, consts_made)
                        wait_apart(pool, stage_in[i], DMA * (ffn * HC // 2 + u + 1), consts_made)
                        split_chunk(i, ffn * HC + 2 * u + i, 2 * u + i)
                with pool.Fori(0, HC // 2) as u:
                    two(u)

            for i in range(2):
                pool.wait_ge(xf_out[i], DMA * NT // 2)
            gather_rows(SHARED, 1)
            next_chunks(1, SHARED - 1)
            gather_rows(SHARED + 1, 2)
            gather_res(SHARED, 3)
            t0 = read_t0(pool)

            def slot(s):
                base = 3 + 3 * (s - SHARED - 1)
                gather_rows(s + 1, base + 1)
                scatter_out(s - 1, base + 2)
                gather_res(s, base + 3)

            with pool.If(t0 > 1):
                with pool.Fori(SHARED + 1, SHARED + t0) as s:
                    slot(s)
            next_chunks(2, SHARED - 1 + t0)
            with pool.Fori(SHARED + t0, SLOTS) as s:
                slot(s)
            scatter_out(SLOTS - 1, 4 + 3 * (SLOTS - 1 - SHARED))
            pool.wait_ge(scattered, M * DMA * EXPERT)
            pool.wait_ge(rows_gathered, M * DMA * (EXPERT + 1))

        @block.scalar
        def _(act):
            act.wait_ge(const_in, 4 * DMA)
            act.wait_ge(d_step, 2)
            nc.scalar.activation(dcol[:, 2, :], dcol[:, 1, :], ACT.Sqrt).then_inc(root_ready, 1)
            act.wait_ge(d_ready, 2)
            nc.scalar.copy(d1_row, y_ps[1][:]).then_inc(d1_row_ready, 1)

            def split_hi(t, i):
                act.wait_ge(ring_in[i], DMA * (t + 1))
                wait(act, tile_mm, RING * t + i + 1 - RING)
                nc.scalar.copy(x_hi[:, :, i * P:(i + 1) * P],
                               ring[:, i, :].rearrange("p (k n) -> p k n", k=KD)).then_inc(tile_hi, 1)

            def take_xf(t, i):
                c = RING * t + i
                act.wait_ge(tile_mm, c + 1)
                wait(act, gate_done, c - 1)
                wait(act, xf_out[i % 2], DMA * (2 * t + i // 2))
                nc.scalar.copy(xo[:, i % 2, :], h_ps[i % 2][:]).then_inc(xf_ready, 1)

            def tiles_round(t, last):
                for i in range(RING):
                    if i < 2:
                        split_hi(t, i + 2)
                    elif not last:
                        split_hi(t + 1, i - 2)
                    take_xf(t, i)

            split_hi(0, 0)
            split_hi(0, 1)
            tiles_round(0, False)
            with act.Fori(1, ROUNDS - 1) as t:
                tiles_round(t, False)
            tiles_round(ROUNDS - 1, True)

            def transposed(s):
                for k in range(KD):
                    act.wait_ge(xt_ps, KD * s + k + 1)
                    nc.scalar.copy(x_hi[:, k, :], t_ps[k % 2][:]).then_inc(xt_hi, 1)

            def slot(s, ffn):
                for j in range(HC):
                    n = HC * s + j
                    act.wait_ge(h_mm, n + 1)
                    wait(act, h_ready, n - 1)
                    nc.scalar.activation(hf[:, j % 2, :], h_ps[j % 2][:], ACT.Relu,
                                         bias=b1[:, ffn, j:j + 1]).then_inc(hf_ready, 1)
                transposed(s + 1)

            for i in range(2):
                act.wait_ge(xf_out[i], DMA * NT // 2)
            transposed(0)
            slot(0, 0)
            act.wait_ge(soft_in, 3)
            nc.scalar.activation(soft[:, 3:5, :], soft[:, 1:3, :], ACT.Exp).then_inc(soft_exp, 1)
            act.wait_ge(t0_ready, 1)
            t0 = read_t0(act)
            with act.Fori(1, SHARED) as s:
                slot(s, 0)
            with act.Fori(SHARED, SHARED + t0) as s:
                slot(s, 1)
            with act.Fori(SHARED + t0, SLOTS) as s:
                slot(s, 2)

        @block.vector
        def _(dve):
            dve.wait_ge(const_in, 4 * DMA)
            nc.vector.tensor_scalar(ys[:], cnd[:], float(D) ** -0.5, None, ALU.mult).then_inc(d_step, 1)
            dve.wait_ge(w_raw_in, DMA)
            for k in range(KD):
                last = nc.vector.tensor_tensor(scratch[:, k, :], w_raw[:, k, :], w_raw[:, k, :], ALU.mult)
                last.then_inc(sq_ready, 1)
            dve.wait_ge(d_step, 1)
            nc.vector.tensor_tensor(ys2[:], ys[:], ys[:], ALU.mult).then_inc(sq_ready, 1)
            dve.wait_ge(v_ready, 1)
            v = t_ps[0][:, 0:KD * BATCHES]
            nc.vector.tensor_scalar(dcol[:, 0, :], v, EPS, None, ALU.add).then_inc(v_ready, 1)
            dve.wait_ge(v_ready, 2)
            nc.vector.reciprocal(dcol[:, 1, :], dcol[:, 0, :]).then_inc(d_step, 1)
            dve.wait_ge(root_ready, 1)
            nc.vector.tensor_tensor(dcol[:, 3, :], dcol[:, 2, :], dcol[:, 2, :], ALU.mult).then_inc(d_step, 1)
            dve.wait_ge(d_step, 3)
            nc.vector.tensor_tensor(dcol[:, 3, :], dcol[:, 3, :], dcol[:, 0, :], ALU.mult).then_inc(d_step, 1)
            dve.wait_ge(d_step, 4)
            nc.vector.tensor_scalar(dcol[:, 3, :], dcol[:, 3, :], -0.5, 1.5, ALU.mult, ALU.add).then_inc(d_step, 1)
            dve.wait_ge(d_step, 5)
            nc.vector.tensor_tensor(dcol[:, 2, :], dcol[:, 2, :], dcol[:, 3, :], ALU.mult).then_inc(d_step, 1)
            dve.wait_ge(d_step, 6)
            dve.wait_ge(consts_made, 1)
            for b in range(BATCHES):
                for o in range(KD):
                    col = o * BATCHES + b
                    nc.vector.tensor_scalar(hf[:, b, o * P:(o + 1) * P], ident[:], dcol[:, 2, col:col + 1], None,
                                            ALU.mult).then_inc(diag_ready, 1)
            dve.wait_ge(d_ready, 2)
            for k in range(KD):
                nc.vector.scalar_tensor_tensor(out=hf[:, k % 2, :], in0=w_raw[:, k, :], scalar=ys[:, k, 0:1],
                                               in1=y_ps[0][:], op0=ALU.mult, op1=ALU.mult).then_inc(wc_step, 1)
                dve.wait_ge(wc_step, 2 * k + 1)
                hi = w_hi[:, 12 + k, 512:1024]
                nc.vector.tensor_copy(hi, hf[:, k % 2, :]).then_inc(wc_step, 1)
                dve.wait_ge(wc_step, 2 * k + 2)
                nc.vector.tensor_tensor(w_lo[:, 12 + k, 512:1024], hf[:, k % 2, :], hi.bitcast(F32),
                                        ALU.subtract).then_inc(wc0_ready, 1)

            nc.vector.tensor_scalar(b1_relu[:], b1[:], 0.0, None, ALU.max).then_inc(acc_step, 1)
            dve.wait_ge(pads_out, 2 * DMA)

            def split_lo(t, i):
                dve.wait_ge(tile_hi, RING * t + i + 1)
                x_part = slice(i * P, (i + 1) * P)
                nc.vector.tensor_tensor(x_lo[:, :, x_part], ring[:, i, :].rearrange("p (k n) -> p k n", k=KD),
                                        x_hi[:, :, x_part].bitcast(F32), ALU.subtract).then_inc(tile_lo, 1)

            def gate_scores(t, i):
                c = RING * t + i
                dve.wait_ge(xf_ready, c + 1)
                if i == 0:
                    wait(dve, score_kept, t)
                for e in range(2):
                    wait(dve, gate_half if e else gate_done, c + e)
                    nc.vector.tensor_tensor_reduce(out=junk[:], in0=xo[:, i % 2, :], in1=gate_w[:, e, :], scale=1.0,
                                                   scalar=0.0, op0=ALU.mult, op1=ALU.add,
                                                   accum_out=score4[:, e, i:i + 1]).then_inc(gate_done if e else gate_half, 1)
                if i == RING - 1:
                    dve.wait_ge(gate_done, c + 1)
                    nc.vector.tensor_copy(columns(score, t).rearrange("p a e i -> p (a e) i"), score4[:]).then_inc(score_kept, 1)

            def tiles_round(t, last):
                for i in range(RING):
                    if i < 2:
                        split_lo(t, i + 2)
                    elif not last:
                        split_lo(t + 1, i - 2)
                    gate_scores(t, i)

            split_lo(0, 0)
            split_lo(0, 1)
            tiles_round(0, False)
            with dve.Fori(1, ROUNDS - 1) as t:
                tiles_round(t, False)
            tiles_round(ROUNDS - 1, True)
            dve.wait_ge(wc1_step, KD + 3)
            nc.vector.memset(acc, 0.0).then_inc(acc_step, 1)

            def transposed(s):
                for k in range(KD):
                    dve.wait_ge(xt_hi, KD * s + k + 1)
                    nc.vector.tensor_tensor(x_lo[:, k, :], t_ps[k % 2][:], x_hi[:, k, :].bitcast(F32),
                                            ALU.subtract).then_inc(xt_lo, 1)

            def slot(s, ffn):
                for j in range(HC):
                    n = HC * s + j
                    dve.wait_ge(hf_ready, n + 1)
                    wait(dve, y_mm, n - 1)
                    nc.vector.tensor_copy(h_hi[:, j % 2, :], hf[:, j % 2, :]).then_inc(hh_ready, 1)
                    dve.wait_ge(hh_ready, n + 1)
                    nc.vector.tensor_tensor(h_lo[:, j % 2, :], hf[:, j % 2, :], h_hi[:, j % 2, :].bitcast(F32),
                                            ALU.subtract).then_inc(h_ready, 1)
                    if ffn == 0 and j in (3, 10):
                        ch = 2 * s + (0 if j == 3 else 1)
                        dve.wait_ge(aux_in, DMA * (ch + 1))
                        dve.wait_ge(acc_step, 2 + 2 * ch)
                        for e in range(2):
                            nc.vector.scalar_tensor_tensor(out=acc[:, e, :], in0=aux[:, e, :],
                                                           scalar=columns(b1_relu[:, 1 + e, :], ch), in1=acc[:, e, :],
                                                           op0=ALU.mult, op1=ALU.add).then_inc(acc_step, 1)
                    if j in (6, 8, 12, 14):
                        m = (6, 8, 12, 14).index(j)
                        if ffn == 0:
                            dve.wait_ge(res_in, DMA * (s + 1))
                        else:
                            dve.wait_ge(res_gathered, M * DMA * (s - SHARED + 1))
                        nc.vector.tensor_tensor(res[:, m, :], res[:, m, :], bias[:, ffn, :], ALU.add).then_inc(res_biased, 1)
                transposed(s + 1)
                for m in range(M):
                    dve.wait_ge(y_mm, HC * (s + 1))
                    dve.wait_ge(res_biased, M * s + m + 1)
                    nc.vector.tensor_tensor(res[:, m, :], y_ps[m][:], res[:, m, :], ALU.add).then_inc(out_ready, 1)

            transposed(0)
            slot(0, 0)

            r = [0]

            def step(ins):
                r[0] += 1
                ins.then_inc(route, 1)
                dve.wait_ge(route, r[0])

            dve.wait_ge(score_kept, ROUNDS)

            def cols(ap):
                return ap.rearrange("p (t i) -> p t i", i=RING)

            g0, g1 = score[:, :, 0, :], score[:, :, 1, :]
            nc.vector.tensor_tensor(cols(soft[:, 0, :]), g0, g1, ALU.max).then_inc(soft_in, 1)
            dve.wait_ge(soft_in, 1)
            nc.vector.tensor_tensor(cols(soft[:, 1, :]), g0, cols(soft[:, 0, :]), ALU.subtract).then_inc(soft_in, 1)
            nc.vector.tensor_tensor(cols(soft[:, 2, :]), g1, cols(soft[:, 0, :]), ALU.subtract).then_inc(soft_in, 1)
            dve.wait_ge(soft_exp, 1)
            step(nc.vector.tensor_tensor(soft[:, 5, :], soft[:, 3, :], soft[:, 4, :], ALU.add))
            step(nc.vector.reciprocal(soft[:, 6, :], soft[:, 5, :]))
            step(nc.vector.tensor_tensor(soft[:, 0, :], soft[:, 3, :], soft[:, 6, :], ALU.mult))
            step(nc.vector.tensor_tensor(soft[:, 7, :], soft[:, 4, :], soft[:, 6, :], ALU.mult))
            nc.vector.tensor_tensor(pick0[:], soft[:, 0, :], soft[:, 7, :], ALU.is_ge).then_inc(pick_ready, 1)
            dve.wait_ge(rank_ps, 1)
            step(nc.vector.tensor_copy(rank[:], t_ps[0][:, 0:2 * NT].rearrange("p (a c) -> p a c", a=2)))
            step(nc.vector.tensor_copy(scan[:, 0, :], rank[:, 1, :]))
            a = 0
            for sh in (1, 2, 4, 8, 16):
                r[0] += 1
                nc.vector.tensor_copy(scan[:, 1 - a, 0:sh], scan[:, a, 0:sh]).then_inc(route, 1)
                step(nc.vector.tensor_tensor(scan[:, 1 - a, sh:NT], scan[:, a, sh:NT], scan[:, a, 0:NT - sh], ALU.add))
                a = 1 - a
            total = scan[:, a, NT - 1:NT]
            step(nc.vector.tensor_scalar(over[:, 1:8], steps[:, 1:8], total, None, ALU.is_lt))
            step(nc.vector.reduce_sum(t0_f[:, 0:1], over[:, 1:SHARED], AX.X))
            step(nc.vector.tensor_scalar(t0_f[:, 1:2], t0_f[:, 0:1], 1.0, None, ALU.add))
            nc.vector.tensor_copy(t0_i[:], t0_f[:, 1:2]).then_inc(t0_ready, 1)
            step(nc.vector.tensor_scalar(over[:, 0:1], t0_f[:, 1:2], float(T), None, ALU.mult))
            step(nc.vector.tensor_tensor(place[:, 0, :], scan[:, a, :], rank[:, 1, :], ALU.subtract))
            step(nc.vector.tensor_tensor(place[:, 1, :], place[:, 0, :], rank[:, 0, :], ALU.add))
            step(nc.vector.tensor_tensor(place[:, 2, :], order[:], place[:, 1, :], ALU.subtract))
            step(nc.vector.tensor_scalar(place[:, 2, :], place[:, 2, :], over[:, 0:1], None, ALU.add))
            step(nc.vector.tensor_tensor(place[:, 3, :], place[:, 1, :], place[:, 2, :], ALU.subtract))
            step(nc.vector.tensor_tensor(place[:, 3, :], place[:, 3, :], pick0[:], ALU.mult))
            nc.vector.tensor_tensor(pos[:], place[:, 2, :], place[:, 3, :], ALU.add).then_inc(pos_ready, 1)

            dve.wait_ge(t0_ready, 1)
            t0 = read_t0(dve)
            with dve.Fori(1, SHARED) as s:
                slot(s, 0)
            dve.wait_ge(bias_ps, 1)
            dve.wait_ge(const_in, 6 * DMA)
            nc.vector.tensor_tensor(junk[:], aux[:, 0, :], aux[:, 1, :], ALU.add).then_inc(bias_step, 1)
            dve.wait_ge(bias_step, 1)
            for e in range(2):
                nc.vector.tensor_tensor(bias[:, 1 + e, :], t_ps[1 - e][:], junk[:], ALU.add).then_inc(bias_step, 1)
            dve.wait_ge(bias_step, 3)
            with dve.Fori(SHARED, SHARED + t0) as s:
                slot(s, 1)
            with dve.Fori(SHARED + t0, SLOTS) as s:
                slot(s, 2)

        @block.tensor
        def _(pe):
            pe.wait_ge(sq_ready, KD + 1)
            for o in range(KD):
                for k in range(KD):
                    last = nc.tensor.matmul(t_ps[0][:, o * BATCHES:(o + 1) * BATCHES], scratch[:, k, o * P:(o + 1) * P],
                                            ys2[:, k, :], start=(k == 0), stop=(k == KD - 1))
            last.then_inc(v_ready, 1)
            pe.wait_ge(consts_made, 4)
            for b in range(BATCHES):
                pe.wait_ge(diag_ready, KD * (b + 1))
                for o in range(KD):
                    part = slice(o * P, (o + 1) * P)
                    last = nc.tensor.matmul(y_ps[b][:, part], ones[:], hf[:, b, part], start=True, stop=True)
                last.then_inc(d_ready, 1)

            def project(t, i, b):
                c = RING * t + i
                pe.wait_ge(tile_lo, c + 1)
                wait(pe, xf_ready, c - 1)
                part = slice(i * P, (i + 1) * P)
                for k in range(KD):
                    if b == 0 and isinstance(t, int):
                        pe.wait_ge(wc0_ready, k + 1)
                    w = 12 - 4 * b + k
                    for q, (lhs, rhs) in enumerate(((x_hi, w_hi), (x_hi, w_lo), (x_lo, w_hi))):
                        last = nc.tensor.matmul(h_ps[i % 2][:], lhs[:, k, part], rhs[:, w, 512:1024],
                                                start=(k == 0 and q == 0), stop=(k == KD - 1 and q == 2))
                last.then_inc(tile_mm, 1)

            for i in range(RING):
                project(0, i, 0)
            with pe.Fori(1, ROUNDS // 2) as t:
                for i in range(RING):
                    project(t, i, 0)
            pe.wait_ge(wc1_step, KD + 3)
            with pe.Fori(ROUNDS // 2, ROUNDS) as t:
                for i in range(RING):
                    project(t, i, 1)

            def transpose(s, gathered):
                if gathered:
                    pe.wait_ge(rows_gathered, M * DMA * (s - SHARED + 1))
                else:
                    pe.wait_ge(rows_in, DMA * (s + 1))
                for k in range(KD):
                    wait(pe, xt_lo, KD * s + k - 1)
                    for m in range(M):
                        last = nc.tensor.transpose(t_ps[k % 2][:, m * P:(m + 1) * P], rows[:, m, k * P:(k + 1) * P], ident[:])
                    last.then_inc(xt_ps, 1)

            def hidden(s, ffn, j):
                n = HC * s + j
                if j == 0:
                    pe.wait_ge(xt_lo, KD * (s + 1))
                pe.wait_ge(w_ready, HC * ffn + j + 1)
                wait(pe, hf_ready, n - 1)
                for k in range(KD):
                    part = slice(k * P, (k + 1) * P)
                    for q, (lhs, rhs) in enumerate(((w_hi, x_hi), (w_hi, x_lo), (w_lo, x_hi))):
                        last = nc.tensor.matmul(h_ps[j % 2][:], lhs[:, j, part], rhs[:, k, :],
                                                start=(k == 0 and q == 0), stop=(k == KD - 1 and q == 2))
                last.then_inc(h_mm, 1)

            def down(s, j):
                n = HC * s + j
                pe.wait_ge(h_ready, n + 1)
                for m in range(M):
                    if j == 0:
                        wait(pe, out_ready, M * (s - 1) + m + 1)
                    part = slice(m * P, (m + 1) * P)
                    for q, (lhs, rhs) in enumerate(((h_hi, w_hi), (h_hi, w_lo), (h_lo, w_hi))):
                        last = nc.tensor.matmul(y_ps[m][:], lhs[:, j % 2, part], rhs[:, j, 512:1024],
                                                start=(j == 0 and q == 0), stop=(j == HC - 1 and q == 2))
                last.then_inc(y_mm, 1)

            def slot(s, ffn, next_gathered):
                hidden(s, ffn, 0)
                for j in range(1, HC):
                    hidden(s, ffn, j)
                    if j < HC - 1:
                        down(s, j - 1)
                transpose(s + 1, next_gathered)
                down(s, HC - 2)
                down(s, HC - 1)

            transpose(0, False)
            slot(0, 0, False)
            pe.wait_ge(pick_ready, 1)
            pe.wait_ge(xt_lo, KD * 2)
            nc.tensor.matmul(t_ps[0][:, 0:NT], before[:], pick0[:], start=True, stop=True)
            nc.tensor.matmul(t_ps[0][:, NT:2 * NT], ones[:], pick0[:], start=True, stop=True).then_inc(rank_ps, 1)
            pe.wait_ge(t0_ready, 1)
            t0 = read_t0(pe)
            with pe.Fori(1, SHARED - 1) as s:
                slot(s, 0, False)
            slot(SHARED - 1, 0, True)
            pe.wait_ge(acc_step, 2 + 2 * HC)
            pe.wait_ge(xt_lo, KD * (SHARED + 1))
            for e in range(2):
                last = nc.tensor.matmul(t_ps[e][:], ones[:], acc[:, e, :], start=True, stop=True)
            last.then_inc(bias_ps, 1)
            with pe.Fori(SHARED, SHARED + t0) as s:
                slot(s, 1, True)
            with pe.Fori(SHARED + t0, SLOTS) as s:
                slot(s, 2, True)


def kernel(x, cond_1024, L0_cond_weight, L0_ffn_gate_w, L0_ffn_w1, L0_ffn_b1, L0_ffn_w2, L0_ffn_b2,
           L0_ffn_sw1, L0_ffn_sb1, L0_ffn_sw2, L0_ffn_sb2):
    import numpy as np
    import concourse.bacc as bacc
    from concourse.bass_utils import run_bass_kernel_spmd

    def lay(a):
        return np.ascontiguousarray(a)

    x, cond, w_cond, gate = (np.asarray(a) for a in (x, cond_1024, L0_cond_weight, L0_ffn_gate_w))
    w1, b1, w2, b2 = (np.asarray(a) for a in (L0_ffn_w1, L0_ffn_b1, L0_ffn_w2, L0_ffn_b2))
    sw1, sb1, sw2, sb2 = (np.asarray(a) for a in (L0_ffn_sw1, L0_ffn_sb1, L0_ffn_sw2, L0_ffn_sb2))
    rows = x.reshape(N, D)
    up = np.stack([sw1, w1[0], w1[1]]).reshape(3, KD, P, HC, P).transpose(0, 3, 2, 1, 4).reshape(3 * HC, P, D)
    down = np.stack([sw2, w2[0], w2[1]]).reshape(3 * HC, P, D)
    arrays = {
        "x_rows": lay(rows),
        "x_cols": lay(rows.reshape(NT, P, KD, P).transpose(0, 3, 2, 1).reshape(NT, P, D)),
        "cond": lay(cond.reshape(BATCHES, KD, P).transpose(2, 1, 0)),
        "w_cond": lay(w_cond.reshape(KD, P, D).transpose(1, 0, 2)),
        "w_pack": lay(np.concatenate([up, down], axis=2)),
        "b1_pack": lay(np.stack([sb1, b1[0], b1[1]]).reshape(3, HC, P).transpose(2, 0, 1)),
        "b2_rows": lay(np.stack([sb2, b2[0], b2[1]])),
        "gate": lay(gate),
    }
    nc = bacc.Bacc("TRN2", target_bir_lowering=False, num_devices=1)
    args = [nc.dram_tensor(n, a.shape, mybir.dt.from_np(a.dtype), kind="ExternalInput").ap() for n, a in arrays.items()]
    out = nc.dram_tensor("out", (N, D), F32, kind="ExternalOutput").ap()
    build(nc, *args, out)
    r = run_bass_kernel_spmd(nc, [arrays], core_ids=[0])
    return r.results[0]["out"].reshape(x.shape)
```

```python
from contextlib import ExitStack

import concourse.bass as bass
from concourse import mybir

F32 = mybir.dt.float32
F32R = mybir.dt.float32r
I32 = mybir.dt.int32
ALU = mybir.AluOpType
ACT = mybir.ActivationFunctionType
AX = mybir.AxisListType

P = 128
N = 4096
D = 512
H = 2048
KD = D // P
HC = H // P
T = 512
TE = 256
M = T // P
ME = TE // P
NT = N // P
RING = 4
ROUNDS = NT // RING
BATCHES = 2
SHARED = N // T
EXPERT = N // TE + 1
T0_MAX = EXPERT - 1
SLOTS = SHARED + EXPERT
COLS = (EXPERT + 1) * ME
HB = 3
HALVES = 2 * HC
STAGE = 4
IDW = 16
PAD = N
EPS = 1e-8
DMA = 16


def wait(eng, sem, value):
    if isinstance(value, int) and value <= 0:
        return
    eng.wait_ge(sem, value)


def wait_apart(eng, sem, value, held):
    if not isinstance(value, int):
        value = eng.snap(value)
        eng.wait_ge(held, 1)
    eng.wait_ge(sem, value)


def block_of(ap, i):
    return ap[i] if isinstance(i, int) else ap[bass.ds(i, 1)].rearrange("a p n -> (a p) n")


def columns(ap, i, n=1):
    return ap[:, i:i + n] if isinstance(i, int) else ap[:, bass.ds(i, n)]


def chunk(ap, j):
    return columns(ap, j).rearrange("p a n -> p (a n)")


def token_rows(ap, n0, n):
    return ap[n0:n0 + n, :] if isinstance(n0, int) else ap[bass.ds(n0, n), :]


def slot_rows(ap, s):
    return token_rows(ap, s * T, T).rearrange("(m p) n -> p m n", p=P)


WIDE = (1, T)
NARROW = (2, TE)


def until(s, kind, shared, expert):
    return shared * s if kind is WIDE else SHARED * shared + (s - SHARED) * expert


def build(nc, x_rows, x_cols, cond, w_cond, w_pack, b1_pack, b2_rows, gate, out):
    xf_dram = nc.dram_tensor("xf_scratch", (N, D), F32).ap()
    part_dram = nc.dram_tensor("partial_scratch", (N, D), F32).ap()
    table_dram = nc.dram_tensor("token_table", (COLS * P, IDW), I32).ap()

    with ExitStack() as ctx:
        def sb(name, shape, dt=F32):
            return ctx.enter_context(nc.sbuf_tensor(name, shape, dt))

        def pb(name):
            return ctx.enter_context(nc.psum_tensor(name, [P, 512], F32))

        def sem(name):
            return ctx.enter_context(nc.semaphore(name))

        w_hi = sb("w_hi", [P, HC, 1024], F32R)
        w_lo = sb("w_lo", [P, HC, 1024], F32R)
        stage = sb("stage", [P, STAGE, D])
        rows = sb("rows", [P, M, D])
        res = sb("res", [P, M, D])
        x_hi = sb("x_hi", [P, KD, T], F32R)
        x_lo = sb("x_lo", [P, KD, T], F32R)
        hf = sb("hf", [P, 2, T])
        h_hi = sb("h_hi", [P, HB, T], F32R)
        h_lo = sb("h_lo", [P, HB, T], F32R)
        scratch = sb("scratch", [P, 4, D])
        bias = sb("bias", [P, 3, D])
        gate_w = sb("gate_w", [P, 2, D])
        ident = sb("ident", [P, P])
        ones = sb("ones", [P, P])
        before = sb("before", [P, P])
        b1 = sb("b1", [P, 3, HC])
        b1_relu = sb("b1_relu", [P, 3, HC])
        cnd = sb("cnd", [P, KD, BATCHES])
        ys = sb("ys", [P, KD, BATCHES])
        ys2 = sb("ys2", [P, KD, BATCHES])
        dcol = sb("dcol", [P, 4, KD * BATCHES])
        score4 = sb("score4", [P, 2, RING])
        score = sb("score", [P, ROUNDS, 2, RING])
        soft = sb("soft", [P, 8, NT])
        pick0 = sb("pick0", [P, NT])
        rank = sb("rank", [P, 2, NT])
        scan = sb("scan", [P, 2, NT])
        place = sb("place", [P, 4, NT])
        order = sb("order", [P, NT])
        steps = sb("steps", [P, EXPERT - 1])
        over = sb("over", [P, EXPERT - 1])
        t0_f = sb("t0_f", [P, 2])
        t0_i = sb("t0_i", [P, 1], I32)
        pos = sb("pos", [P, NT], I32)
        tab = sb("tab", [P, COLS], I32)
        tab_in = sb("tab_in", [P, COLS], I32)
        idx_rows = sb("idx_rows", [P, ME], I32)
        idx_res = sb("idx_res", [P, ME], I32)
        idx_out = sb("idx_out", [P, ME], I32)

        w_raw = rows
        ring = res
        xo = hf
        junk = bias[:, 1, :]
        acc = scratch[:, 0:2, :]
        aux = scratch[:, 2:4, :]
        ids = gate_w[:, :, :].rearrange("p e n -> p (e n)")[:, 0:NT * IDW].bitcast(I32)
        pads = junk[:, 0:COLS * IDW // 2].bitcast(I32)

        y_ps = [pb(f"y_ps{m}") for m in range(M)]
        h_ps = [pb(f"h_ps{i}") for i in range(2)]
        t_ps = [pb(f"t_ps{i}") for i in range(2)]

        const_in = sem("const_in")
        gate_in = sem("gate_in")
        w_raw_in = sem("w_raw_in")
        ring_in = [sem(f"ring_in{i}") for i in range(RING)]
        stage_in = [sem(f"stage_in{i}") for i in range(STAGE)]
        rows_in = sem("rows_in")
        res_in = sem("res_in")
        rows_gathered = sem("rows_gathered")
        res_gathered = sem("res_gathered")
        aux_in = sem("aux_in")
        consts_made = sem("consts_made")
        sq_ready = sem("sq_ready")
        v_ready = sem("v_ready")
        d_step = sem("d_step")
        root_ready = sem("root_ready")
        diag_ready = sem("diag_ready")
        d_ready = sem("d_ready")
        wc_step = sem("wc_step")
        wc0_ready = sem("wc0_ready")
        wc1_scaled = sem("wc1_scaled")
        wc1_hi = sem("wc1_hi")
        wc1_ready = sem("wc1_ready")
        tile_hi = sem("tile_hi")
        tile_lo = sem("tile_lo")
        tile_mm = sem("tile_mm")
        xf_ready = sem("xf_ready")
        xf_out = [sem(f"xf_out{i}") for i in range(2)]
        gate_half = sem("gate_half")
        gate_done = sem("gate_done")
        score_kept = sem("score_kept")
        route = sem("route")
        soft_in = sem("soft_in")
        soft_exp = sem("soft_exp")
        pick_ready = sem("pick_ready")
        rank_ps = sem("rank_ps")
        t0_ready = sem("t0_ready")
        pos_ready = sem("pos_ready")
        pads_made = sem("pads_made")
        pads_out = sem("pads_out")
        ids_made = sem("ids_made")
        ids_out = sem("ids_out")
        tab_dma = sem("tab_dma")
        tab_ready = sem("tab_ready")
        idx_made = sem("idx_made")
        w_hi_ready = sem("w_hi_ready")
        w_ready = sem("w_ready")
        xt_ps = sem("xt_ps")
        xt_hi = sem("xt_hi")
        xt_lo = sem("xt_lo")
        h_mm = sem("h_mm")
        hf_ready = sem("hf_ready")
        hh_ready = sem("hh_ready")
        h_ready = sem("h_ready")
        y_mm = sem("y_mm")
        res_biased = sem("res_biased")
        out_ready = sem("out_ready")
        part_out = sem("part_out")
        scattered = sem("scattered")
        acc_step = sem("acc_step")
        bias_ps = sem("bias_ps")
        bias_step = sem("bias_step")

        def read_t0(eng):
            return eng.value_load(t0_i[0:1, 0:1], min_val=1, max_val=T0_MAX)

        block = ctx.enter_context(nc.Block())

        @block.sync
        def _(sp):
            for k in range(KD):
                sp.dma_start(w_raw[:, k, :], w_cond[:, k, :]).then_inc(w_raw_in, DMA)
            sp.dma_start(cnd[:], cond).then_inc(const_in, DMA)
            for i in range(RING):
                sp.dma_start(ring[:, i, :], x_cols[i]).then_inc(ring_in[i], DMA)
            sp.dma_start(gate_w[:], gate.partition_broadcast(P)).then_inc(gate_in, DMA)
            sp.dma_start(b1[:], b1_pack).then_inc(const_in, DMA)
            sp.dma_start(bias[:, 0, :], b2_rows[0].partition_broadcast(P)).then_inc(const_in, DMA)
            for i in range(STAGE):
                sp.dma_start(stage[:, i, :], w_pack[i]).then_inc(stage_in[i], DMA)

            def weight_halves(u):
                for i in range(STAGE):
                    sp.wait_ge(w_ready, STAGE * (u - 1) + i + 1)
                    sp.dma_start(stage[:, i, :], block_of(w_pack, STAGE * u + i)).then_inc(stage_in[i], DMA)

            def tiles_round(t, more):
                for i in range(RING):
                    c = t * RING + i
                    sp.wait_ge(xf_ready, c + 1)
                    sp.dma_start(token_rows(xf_dram, c * P, P), xo[:, i % 2, :]).then_inc(xf_out[i % 2], DMA)
                    if more:
                        sp.wait_ge(tile_lo, c + 1)
                        sp.dma_start(ring[:, i, :], block_of(x_cols, c + RING)).then_inc(ring_in[i], DMA)

            with sp.Fori(0, ROUNDS // 2) as t:
                tiles_round(t, True)
            for i in range(2):
                sp.wait_ge(xf_out[i], 2 * DMA)
            sp.wait_ge(wc1_ready, KD)
            sp.dma_start(rows[:], slot_rows(xf_dram, 0)).then_inc(rows_in, DMA)
            with sp.Fori(ROUNDS // 2, ROUNDS - 1) as t:
                tiles_round(t, True)
            tiles_round(ROUNDS - 1, False)

            sp.wait_ge(tile_lo, NT)
            sp.dma_start(res[:], slot_rows(x_rows, 0)).then_inc(res_in, DMA)

            w2_pair = w_pack.rearrange("(f j h) p n -> h j p f n", f=3, h=2)[1, :, :, 1:3, :]

            def aux_load(j):
                sp.wait_ge(acc_step, 2 + 2 * j)
                src = w2_pair[j] if isinstance(j, int) else w2_pair[bass.ds(j, 1)].rearrange("a p f n -> (a p) f n")
                sp.dma_start(aux, src).then_inc(aux_in, DMA)

            def next_rows(s):
                sp.wait_ge(xt_ps, KD * (s + 1))
                sp.dma_start(rows[:], slot_rows(xf_dram, s + 1)).then_inc(rows_in, DMA)

            def store(s):
                for m in range(M):
                    sp.wait_ge(out_ready, M * s + m + 1)
                    sp.dma_start(token_rows(part_dram, (M * s + m) * P, P), res[:, m, :]).then_inc(part_out, DMA)

            def next_res(s):
                sp.wait_ge(part_out, M * DMA * (s + 1))
                sp.dma_start(res[:], slot_rows(x_rows, s + 1)).then_inc(res_in, DMA)

            aux_load(0)
            for u in range(1, 4):
                weight_halves(u)
            aux_load(1)
            for i in range(2):
                sp.wait_ge(xf_out[i], DMA * NT // 2)
            next_rows(0)
            for u in range(4, HALVES // STAGE + 1):
                weight_halves(u)
            aux_load(2)
            store(0)
            next_res(0)
            with sp.Fori(1, SHARED - 1) as s:
                next_rows(s)
                aux_load(2 * s + 1)
                aux_load(2 * s + 2)
                store(s)
                next_res(s)
            aux_load(HC - 1)
            sp.wait_ge(acc_step, 2 + 2 * HC)
            for e in range(2):
                sp.dma_start(aux[:, e, :], b2_rows[1 + e].partition_broadcast(P)).then_inc(const_in, DMA)
            store(SHARED - 1)
            with sp.Fori(HALVES // STAGE + 1, 3 * HALVES // STAGE) as u:
                weight_halves(u)

        @block.gpsimd
        def _(pool):
            pool.memset(ident[:], 0.0).then_inc(pads_made, 1)
            pool.memset(ones[:], 1.0).then_inc(pads_made, 1)
            pool.memset(pads, PAD).then_inc(pads_made, 1)
            pool.wait_ge(pads_made, 3)
            pool.affine_select(out=ident[:], in_=ident[:], compare_op=ALU.not_equal, fill=1.0, base=0,
                               pattern=[[-1, P]], channel_multiplier=1).then_inc(consts_made, 1)
            pool.affine_select(out=before[:], in_=ones[:], compare_op=ALU.is_gt, fill=0.0, base=0,
                               pattern=[[1, P]], channel_multiplier=-1).then_inc(consts_made, 1)
            pool.iota(order[:], [[P, NT]], base=0, channel_multiplier=1,
                      allow_small_or_imprecise_dtypes=True).then_inc(consts_made, 1)
            pool.iota(steps[:], [[TE, EXPERT - 1]], base=0, channel_multiplier=0,
                      allow_small_or_imprecise_dtypes=True).then_inc(consts_made, 1)
            half = COLS * IDW // 2
            table_p = table_dram.rearrange("(p c) w -> p (c w)", p=P)
            for i in range(2):
                pool.dma_start(table_p[:, i * half:(i + 1) * half], pads).then_inc(pads_out, DMA)

            pool.wait_ge(gate_done, NT)
            pool.iota(ids, [[P, NT], [0, IDW]], base=0, channel_multiplier=1).then_inc(ids_made, 1)
            pool.wait_ge(ids_made, 1)
            pool.wait_ge(pads_out, 2 * DMA)
            pool.wait_ge(pos_ready, 1)
            for c in range(NT):
                pool.indirect_dma_start(table_dram, bass.IndirectOffsetOnAxis(pos[:, c:c + 1], 0),
                                        ids[:, c * IDW:(c + 1) * IDW], None).then_inc(ids_out, DMA)
            pool.wait_ge(ids_out, NT * DMA)
            with nc.allow_non_contiguous_dma(reason="one number per 64-byte row"):
                pool.dma_start(tab[:], table_dram.rearrange("(c p) w -> p c w", p=P)[:, :, 0]).then_inc(tab_dma, DMA)
            pool.wait_ge(tab_dma, DMA)
            pool.tensor_scalar(tab_in[:], tab[:], N - 1, None, ALU.min).then_inc(tab_ready, 1)
            pool.wait_ge(tab_ready, 1)

            def numbers(dst, table, s):
                pool.tensor_copy(dst[:], columns(table, (s - SHARED) * ME, ME)).then_inc(idx_made, 1)
                pool.drain()

            def gather_rows(s):
                wait_apart(pool, xt_ps, until(s, NARROW, KD, KD // 2), tab_ready)
                numbers(idx_rows, tab_in, s)
                for m in range(ME):
                    pool.indirect_dma_start(rows[:, m, :], None, xf_dram,
                                            bass.IndirectOffsetOnAxis(idx_rows[:, m:m + 1], 0)).then_inc(rows_gathered, DMA)

            def gather_res(s):
                if isinstance(s, int):
                    pool.wait_ge(part_out, M * DMA * SHARED)
                else:
                    wait_apart(pool, scattered, ME * DMA * (s - SHARED), tab_ready)
                numbers(idx_res, tab_in, s)
                for m in range(ME):
                    pool.indirect_dma_start(res[:, m, :], None, part_dram,
                                            bass.IndirectOffsetOnAxis(idx_res[:, m:m + 1], 0)).then_inc(res_gathered, DMA)

            def scatter(m):
                pool.indirect_dma_start(out, bass.IndirectOffsetOnAxis(idx_out[:, m:m + 1], 0), res[:, m, :], None,
                                        bounds_check=N - 1, oob_is_err=False).then_inc(scattered, DMA)

            def scatter_out(s):
                wait_apart(pool, out_ready, until(s + 1, NARROW, M, ME), tab_ready)
                numbers(idx_out, tab, s)
                for m in range(ME):
                    scatter(m)

            for i in range(2):
                pool.wait_ge(xf_out[i], DMA * NT // 2)
            gather_rows(SHARED)
            gather_rows(SHARED + 1)
            gather_res(SHARED)
            with pool.Fori(SHARED + 1, SLOTS) as s:
                scatter_out(s - 1)
                gather_rows(s + 1)
                gather_res(s)
            numbers(idx_out, tab, SLOTS - 1)
            for m in range(ME):
                pool.wait_ge(out_ready, until(SLOTS - 1, NARROW, M, ME) + m + 1)
                scatter(m)
            pool.wait_ge(scattered, ME * DMA * EXPERT)
            pool.wait_ge(rows_gathered, ME * DMA * (EXPERT + 1))

        @block.scalar
        def _(act):
            act.wait_ge(d_step, 2)
            nc.scalar.activation(dcol[:, 2, :], dcol[:, 1, :], ACT.Sqrt).then_inc(root_ready, 1)

            def split_hi(t, i):
                act.wait_ge(ring_in[i], DMA * (t + 1))
                wait(act, tile_mm, RING * t + i + 1 - RING)
                nc.scalar.copy(x_hi[:, :, i * P:(i + 1) * P],
                               ring[:, i, :].rearrange("p (k n) -> p k n", k=KD)).then_inc(tile_hi, 1)

            def take_xf(t, i):
                c = RING * t + i
                act.wait_ge(tile_mm, c + 1)
                wait(act, gate_done, c - 1)
                wait(act, xf_out[i % 2], DMA * (2 * t + i // 2))
                nc.scalar.copy(xo[:, i % 2, :], h_ps[i % 2][:]).then_inc(xf_ready, 1)

            def wc1_part(k):
                act.wait_ge(wc1_scaled, k + 1)
                nc.scalar.copy(chunk(w_hi, 8 + k)[:, D:2 * D], chunk(scratch, k)).then_inc(wc1_hi, 1)

            def weights_hi(ffn, j):
                for half in range(2):
                    h = HALVES * ffn + 2 * j + half
                    act.wait_ge(stage_in[h % STAGE], DMA * (h // STAGE + 1))
                    nc.scalar.copy(w_hi[:, j, half * D:(half + 1) * D], stage[:, h % STAGE, :]).then_inc(w_hi_ready, 1)

            def tiles_round(t, last, wc1):
                if wc1:
                    wc1_part(t)
                for i in range(RING):
                    if i < 2:
                        split_hi(t, i + 2)
                    elif not last:
                        split_hi(t + 1, i - 2)
                    if last and i < 2:
                        weights_hi(0, i)
                    take_xf(t, i)

            split_hi(0, 0)
            split_hi(0, 1)
            tiles_round(0, False, True)
            with act.Fori(1, ROUNDS // 2) as t:
                tiles_round(t, False, True)
            with act.Fori(ROUNDS // 2, ROUNDS - 1) as t:
                tiles_round(t, False, False)
            tiles_round(ROUNDS - 1, True, False)

            def transposed(s, kind):
                per_bank, tok = kind
                for f in range(KD // per_bank):
                    act.wait_ge(xt_ps, until(s, kind, KD, KD // 2) + f + 1)
                    nc.scalar.copy(x_hi[:, f * per_bank:(f + 1) * per_bank, 0:tok],
                                   t_ps[f % 2][:].rearrange("p (k n) -> p k n", k=per_bank)).then_inc(xt_hi, 1)

            def slot(s, ffn, first, nxt):
                tok = T if ffn == 0 else TE
                for j in range(HC):
                    n = HC * s + j
                    act.wait_ge(h_mm, n + 1)
                    wait(act, h_ready, n - 1)
                    nc.scalar.activation(hf[:, j % 2, 0:tok], h_ps[j % 2][:, 0:tok], ACT.Relu,
                                         bias=b1[:, ffn, j:j + 1]).then_inc(hf_ready, 1)
                    if first and j + 2 < HC:
                        if j == 0:
                            wait(act, y_mm, HC * s)
                            act.wait_ge(tile_mm, NT)
                        weights_hi(ffn, j + 2)
                    if isinstance(s, int) and s == 0 and j == 2:
                        act.wait_ge(soft_in, 3)
                        nc.scalar.activation(soft[:, 3:5, :], soft[:, 1:3, :], ACT.Exp).then_inc(soft_exp, 1)
                transposed(s + 1, nxt)

            def change(s, ffn):
                act.wait_ge(y_mm, HC * (s - 1) + 2)
                for j in range(2):
                    weights_hi(ffn, j)

            for i in range(2):
                act.wait_ge(xf_out[i], DMA * NT // 2)
            act.wait_ge(const_in, 3 * DMA)
            transposed(0, WIDE)
            slot(0, 0, True, WIDE)
            act.wait_ge(t0_ready, 1)
            t0 = read_t0(act)
            with act.Fori(1, SHARED - 1) as s:
                slot(s, 0, False, WIDE)
            slot(SHARED - 1, 0, False, NARROW)
            change(SHARED, 1)
            slot(SHARED, 1, True, NARROW)
            with act.If(t0 > 1):
                with act.Fori(SHARED + 1, SHARED + t0) as s:
                    slot(s, 1, False, NARROW)
            s1 = act.snap(t0 + SHARED)
            change(s1, 2)
            slot(s1, 2, True, NARROW)
            with act.If(t0 < T0_MAX):
                with act.Fori(SHARED + 1 + t0, SLOTS) as s:
                    slot(s, 2, False, NARROW)

        @block.vector
        def _(dve):
            dve.wait_ge(const_in, 3 * DMA)
            nc.vector.tensor_scalar(ys[:], cnd[:], float(D) ** -0.5, None, ALU.mult).then_inc(d_step, 1)
            dve.wait_ge(d_step, 1)
            nc.vector.tensor_tensor(ys2[:], ys[:], ys[:], ALU.mult).then_inc(sq_ready, 1)
            dve.wait_ge(w_raw_in, KD * DMA)
            for k in range(KD):
                nc.vector.tensor_tensor(scratch[:, k, :], w_raw[:, k, :], w_raw[:, k, :], ALU.mult).then_inc(sq_ready, 1)
            dve.wait_ge(v_ready, 1)
            v = t_ps[0][:, 0:KD * BATCHES]
            nc.vector.tensor_scalar(dcol[:, 0, :], v, EPS, None, ALU.add).then_inc(v_ready, 1)
            dve.wait_ge(v_ready, 2)
            nc.vector.reciprocal(dcol[:, 1, :], dcol[:, 0, :]).then_inc(d_step, 1)
            dve.wait_ge(root_ready, 1)
            nc.vector.tensor_tensor(dcol[:, 3, :], dcol[:, 2, :], dcol[:, 2, :], ALU.mult).then_inc(d_step, 1)
            dve.wait_ge(d_step, 3)
            nc.vector.tensor_tensor(dcol[:, 3, :], dcol[:, 3, :], dcol[:, 0, :], ALU.mult).then_inc(d_step, 1)
            dve.wait_ge(d_step, 4)
            nc.vector.tensor_scalar(dcol[:, 3, :], dcol[:, 3, :], -0.5, 1.5, ALU.mult, ALU.add).then_inc(d_step, 1)
            dve.wait_ge(d_step, 5)
            nc.vector.tensor_tensor(dcol[:, 2, :], dcol[:, 2, :], dcol[:, 3, :], ALU.mult).then_inc(d_step, 1)
            dve.wait_ge(d_step, 6)
            dve.wait_ge(consts_made, 1)
            for b in range(BATCHES):
                for o in range(KD):
                    col = o * BATCHES + b
                    nc.vector.tensor_scalar(hf[:, b, o * P:(o + 1) * P], ident[:], dcol[:, 2, col:col + 1], None,
                                            ALU.mult).then_inc(diag_ready, 1)
            dve.wait_ge(d_ready, 2)
            for k in range(KD):
                nc.vector.scalar_tensor_tensor(out=hf[:, k % 2, :], in0=w_raw[:, k, :], scalar=ys[:, k, 0:1],
                                               in1=y_ps[0][:], op0=ALU.mult, op1=ALU.mult).then_inc(wc_step, 1)
                dve.wait_ge(wc_step, 2 * k + 1)
                hi = w_hi[:, 12 + k, 512:1024]
                nc.vector.tensor_copy(hi, hf[:, k % 2, :]).then_inc(wc_step, 1)
                dve.wait_ge(wc_step, 2 * k + 2)
                nc.vector.tensor_tensor(w_lo[:, 12 + k, 512:1024], hf[:, k % 2, :], hi.bitcast(F32),
                                        ALU.subtract).then_inc(wc0_ready, 1)

            nc.vector.tensor_scalar(b1_relu[:], b1[:], 0.0, None, ALU.max).then_inc(acc_step, 1)
            dve.wait_ge(pads_out, 2 * DMA)
            dve.wait_ge(gate_in, DMA)

            def wc1_part(k):
                nc.vector.scalar_tensor_tensor(out=chunk(scratch, k), in0=chunk(w_raw, k),
                                               scalar=columns(ys[:, :, 1], k), in1=y_ps[1][:], op0=ALU.mult,
                                               op1=ALU.mult).then_inc(wc1_scaled, 1)

            def wc1_rest(k):
                dve.wait_ge(wc1_hi, k + 1)
                nc.vector.tensor_tensor(chunk(w_lo, 8 + k)[:, D:2 * D], chunk(scratch, k),
                                        chunk(w_hi, 8 + k)[:, D:2 * D].bitcast(F32),
                                        ALU.subtract).then_inc(wc1_ready, 1)

            def weights_lo(ffn, j):
                for half in range(2):
                    h = HALVES * ffn + 2 * j + half
                    part = slice(half * D, (half + 1) * D)
                    dve.wait_ge(w_hi_ready, h + 1)
                    nc.vector.tensor_tensor(w_lo[:, j, part], stage[:, h % STAGE, :], w_hi[:, j, part].bitcast(F32),
                                            ALU.subtract).then_inc(w_ready, 1)

            def split_lo(t, i):
                dve.wait_ge(tile_hi, RING * t + i + 1)
                x_part = slice(i * P, (i + 1) * P)
                nc.vector.tensor_tensor(x_lo[:, :, x_part], ring[:, i, :].rearrange("p (k n) -> p k n", k=KD),
                                        x_hi[:, :, x_part].bitcast(F32), ALU.subtract).then_inc(tile_lo, 1)

            def gate_scores(t, i):
                c = RING * t + i
                dve.wait_ge(xf_ready, c + 1)
                if i == 0:
                    wait(dve, score_kept, t)
                for e in range(2):
                    wait(dve, gate_half if e else gate_done, c + e)
                    nc.vector.tensor_tensor_reduce(out=junk, in0=xo[:, i % 2, :], in1=gate_w[:, e, :], scale=1.0,
                                                   scalar=0.0, op0=ALU.mult, op1=ALU.add,
                                                   accum_out=score4[:, e, i:i + 1]).then_inc(gate_done if e else gate_half, 1)
                if i == RING - 1:
                    dve.wait_ge(gate_done, c + 1)
                    nc.vector.tensor_copy(columns(score, t).rearrange("p a e i -> p (a e) i"), score4[:]).then_inc(score_kept, 1)

            def tiles_round(t, last, wc1):
                for i in range(RING):
                    if i < 2:
                        split_lo(t, i + 2)
                    elif not last:
                        split_lo(t + 1, i - 2)
                    if wc1 and i == 1:
                        wc1_rest(t)
                    if wc1 and i == 3 and not (isinstance(t, int) and t == ROUNDS // 2 - 1):
                        wc1_part(t + 1)
                    if last and i < 2:
                        weights_lo(0, i)
                    gate_scores(t, i)

            wc1_part(0)
            split_lo(0, 0)
            split_lo(0, 1)
            tiles_round(0, False, True)
            with dve.Fori(1, ROUNDS // 2 - 1) as t:
                tiles_round(t, False, True)
            tiles_round(ROUNDS // 2 - 1, False, True)
            with dve.Fori(ROUNDS // 2, ROUNDS - 1) as t:
                tiles_round(t, False, False)
            tiles_round(ROUNDS - 1, True, False)
            nc.vector.memset(acc, 0.0).then_inc(acc_step, 1)

            def transposed(s, kind):
                per_bank, tok = kind
                for f in range(KD // per_bank):
                    ks = slice(f * per_bank, (f + 1) * per_bank)
                    dve.wait_ge(xt_hi, until(s, kind, KD, KD // 2) + f + 1)
                    nc.vector.tensor_tensor(x_lo[:, ks, 0:tok], t_ps[f % 2][:].rearrange("p (k n) -> p k n", k=per_bank),
                                            x_hi[:, ks, 0:tok].bitcast(F32), ALU.subtract).then_inc(xt_lo, 1)

            r = [0]

            def step(ins):
                r[0] += 1
                ins.then_inc(route, 1)
                dve.wait_ge(route, r[0])

            def softmax_start():
                def cols(ap):
                    return ap.rearrange("p (t i) -> p t i", i=RING)

                g0, g1 = score[:, :, 0, :], score[:, :, 1, :]
                dve.wait_ge(score_kept, ROUNDS)
                nc.vector.tensor_tensor(cols(soft[:, 0, :]), g0, g1, ALU.max).then_inc(soft_in, 1)
                dve.wait_ge(soft_in, 1)
                nc.vector.tensor_tensor(cols(soft[:, 1, :]), g0, cols(soft[:, 0, :]), ALU.subtract).then_inc(soft_in, 1)
                nc.vector.tensor_tensor(cols(soft[:, 2, :]), g1, cols(soft[:, 0, :]), ALU.subtract).then_inc(soft_in, 1)

            def choose():
                dve.wait_ge(soft_exp, 1)
                step(nc.vector.tensor_tensor(soft[:, 5, :], soft[:, 3, :], soft[:, 4, :], ALU.add))
                step(nc.vector.reciprocal(soft[:, 6, :], soft[:, 5, :]))
                step(nc.vector.tensor_tensor(soft[:, 0, :], soft[:, 3, :], soft[:, 6, :], ALU.mult))
                step(nc.vector.tensor_tensor(soft[:, 7, :], soft[:, 4, :], soft[:, 6, :], ALU.mult))
                nc.vector.tensor_tensor(pick0[:], soft[:, 0, :], soft[:, 7, :], ALU.is_ge).then_inc(pick_ready, 1)

            def count():
                dve.wait_ge(rank_ps, 1)
                step(nc.vector.tensor_copy(rank[:], t_ps[0][:, 0:2 * NT].rearrange("p (a c) -> p a c", a=2)))
                step(nc.vector.tensor_copy(scan[:, 0, :], rank[:, 1, :]))
                a = 0
                for sh in (1, 2, 4, 8, 16):
                    r[0] += 1
                    nc.vector.tensor_copy(scan[:, 1 - a, 0:sh], scan[:, a, 0:sh]).then_inc(route, 1)
                    step(nc.vector.tensor_tensor(scan[:, 1 - a, sh:NT], scan[:, a, sh:NT], scan[:, a, 0:NT - sh], ALU.add))
                    a = 1 - a

            def places():
                total = scan[:, 1, NT - 1:NT]
                step(nc.vector.tensor_scalar(over[:, 1:T0_MAX], steps[:, 1:T0_MAX], total, None, ALU.is_lt))
                step(nc.vector.reduce_sum(t0_f[:, 0:1], over[:, 1:T0_MAX], AX.X))
                step(nc.vector.tensor_scalar(t0_f[:, 1:2], t0_f[:, 0:1], 1.0, None, ALU.add))
                nc.vector.tensor_copy(t0_i[:], t0_f[:, 1:2]).then_inc(t0_ready, 1)
                step(nc.vector.tensor_scalar(over[:, 0:1], t0_f[:, 1:2], float(TE), None, ALU.mult))
                step(nc.vector.tensor_tensor(place[:, 0, :], scan[:, 1, :], rank[:, 1, :], ALU.subtract))
                step(nc.vector.tensor_tensor(place[:, 1, :], place[:, 0, :], rank[:, 0, :], ALU.add))
                step(nc.vector.tensor_tensor(place[:, 2, :], order[:], place[:, 1, :], ALU.subtract))
                step(nc.vector.tensor_scalar(place[:, 2, :], place[:, 2, :], over[:, 0:1], None, ALU.add))
                step(nc.vector.tensor_tensor(place[:, 3, :], place[:, 1, :], place[:, 2, :], ALU.subtract))
                step(nc.vector.tensor_tensor(place[:, 3, :], place[:, 3, :], pick0[:], ALU.mult))
                nc.vector.tensor_tensor(pos[:], place[:, 2, :], place[:, 3, :], ALU.add).then_inc(pos_ready, 1)

            def constant_rows(s, which):
                ch = 2 * s + which
                dve.wait_ge(aux_in, DMA * (ch + 1))
                dve.wait_ge(acc_step, 2 + 2 * ch)
                for e in range(2):
                    nc.vector.scalar_tensor_tensor(out=acc[:, e, :], in0=aux[:, e, :],
                                                   scalar=columns(b1_relu[:, 1 + e, :], ch), in1=acc[:, e, :],
                                                   op0=ALU.mult, op1=ALU.add).then_inc(acc_step, 1)

            def slot(s, ffn, first, nxt):
                tok, groups = (T, M) if ffn == 0 else (TE, ME)
                at_start = isinstance(s, int) and s == 0
                for j in range(HC):
                    n = HC * s + j
                    buf = j % HB
                    dve.wait_ge(hf_ready, n + 1)
                    wait(dve, y_mm, n - HB + 1 if j >= HB else HC * s)
                    nc.vector.tensor_copy(h_hi[:, buf, 0:tok], hf[:, j % 2, 0:tok]).then_inc(hh_ready, 1)
                    dve.wait_ge(hh_ready, n + 1)
                    nc.vector.tensor_tensor(h_lo[:, buf, 0:tok], hf[:, j % 2, 0:tok], h_hi[:, buf, 0:tok].bitcast(F32),
                                            ALU.subtract).then_inc(h_ready, 1)
                    if first and j + 2 < HC:
                        weights_lo(ffn, j + 2)
                    if ffn == 0 and j in (3, 10):
                        constant_rows(s, 0 if j == 3 else 1)
                    if j in (8, 12, 13, 14)[:groups]:
                        m = (8, 12, 13, 14).index(j)
                        if ffn == 0:
                            dve.wait_ge(res_in, DMA * (s + 1))
                        else:
                            dve.wait_ge(res_gathered, ME * DMA * (s - SHARED + 1))
                        nc.vector.tensor_tensor(res[:, m, :], res[:, m, :], bias[:, ffn, :], ALU.add).then_inc(res_biased, 1)
                    if at_start and j == 1:
                        softmax_start()
                    if at_start and j == 4:
                        choose()
                    if at_start and j == 7:
                        count()
                    if at_start and j == 9:
                        places()
                transposed(s + 1, nxt)
                for m in range(groups):
                    dve.wait_ge(y_mm, HC * (s + 1))
                    dve.wait_ge(res_biased, until(s, WIDE if ffn == 0 else NARROW, M, ME) + m + 1)
                    nc.vector.tensor_tensor(res[:, m, :], y_ps[m][:], res[:, m, :], ALU.add).then_inc(out_ready, 1)

            transposed(0, WIDE)
            slot(0, 0, True, WIDE)
            dve.wait_ge(t0_ready, 1)
            t0 = read_t0(dve)
            with dve.Fori(1, SHARED - 1) as s:
                slot(s, 0, False, WIDE)
            slot(SHARED - 1, 0, False, NARROW)

            def change(ffn):
                for j in range(2):
                    weights_lo(ffn, j)

            change(1)
            dve.wait_ge(bias_ps, 1)
            dve.wait_ge(const_in, 5 * DMA)
            nc.vector.tensor_tensor(bias[:, 1, :], aux[:, 0, :], aux[:, 1, :], ALU.add).then_inc(bias_step, 1)
            dve.wait_ge(bias_step, 1)
            for e in (1, 0):
                nc.vector.tensor_tensor(bias[:, 1 + e, :], t_ps[1 - e][:], bias[:, 1, :], ALU.add).then_inc(bias_step, 1)
            dve.wait_ge(bias_step, 3)
            slot(SHARED, 1, True, NARROW)
            with dve.If(t0 > 1):
                with dve.Fori(SHARED + 1, SHARED + t0) as s:
                    slot(s, 1, False, NARROW)
            change(2)
            slot(dve.snap(t0 + SHARED), 2, True, NARROW)
            with dve.If(t0 < T0_MAX):
                with dve.Fori(SHARED + 1 + t0, SLOTS) as s:
                    slot(s, 2, False, NARROW)

        @block.tensor
        def _(pe):
            pe.wait_ge(sq_ready, KD + 1)
            for o in range(KD):
                for k in range(KD):
                    last = nc.tensor.matmul(t_ps[0][:, o * BATCHES:(o + 1) * BATCHES], scratch[:, k, o * P:(o + 1) * P],
                                            ys2[:, k, :], start=(k == 0), stop=(k == KD - 1))
            last.then_inc(v_ready, 1)
            pe.wait_ge(consts_made, 4)
            for b in range(BATCHES):
                pe.wait_ge(diag_ready, KD * (b + 1))
                for o in range(KD):
                    part = slice(o * P, (o + 1) * P)
                    last = nc.tensor.matmul(y_ps[b][:, part], ones[:], hf[:, b, part], start=True, stop=True)
                last.then_inc(d_ready, 1)

            def project(t, i, b):
                c = RING * t + i
                pe.wait_ge(tile_lo, c + 1)
                wait(pe, xf_ready, c - 1)
                part = slice(i * P, (i + 1) * P)
                for k in range(KD):
                    if b == 0 and isinstance(t, int):
                        pe.wait_ge(wc0_ready, k + 1)
                    w = 12 - 4 * b + k
                    for q, (lhs, rhs) in enumerate(((x_hi, w_hi), (x_hi, w_lo), (x_lo, w_hi))):
                        last = nc.tensor.matmul(h_ps[i % 2][:], lhs[:, k, part], rhs[:, w, 512:1024],
                                                start=(k == 0 and q == 0), stop=(k == KD - 1 and q == 2))
                last.then_inc(tile_mm, 1)

            for i in range(RING):
                project(0, i, 0)
            with pe.Fori(1, ROUNDS // 2) as t:
                for i in range(RING):
                    project(t, i, 0)
            pe.wait_ge(wc1_ready, KD)
            with pe.Fori(ROUNDS // 2, ROUNDS) as t:
                for i in range(RING):
                    project(t, i, 1)

            def transpose(s, kind, banks):
                per_bank, tok = kind
                if kind is WIDE:
                    pe.wait_ge(rows_in, DMA * (s + 1))
                else:
                    pe.wait_ge(rows_gathered, ME * DMA * (s - SHARED + 1))
                for f in banks:
                    wait(pe, xt_lo, until(s, kind, KD, KD // 2) + f - 1)
                    for q in range(per_bank):
                        k = f * per_bank + q
                        for m in range(tok // P):
                            at = q * tok + m * P
                            last = nc.tensor.transpose(t_ps[f % 2][:, at:at + P], rows[:, m, k * P:(k + 1) * P], ident[:])
                    last.then_inc(xt_ps, 1)

            def hidden(s, ffn, j, kind):
                tok = kind[1]
                n = HC * s + j
                if j == 0:
                    pe.wait_ge(xt_lo, until(s + 1, kind, KD, KD // 2))
                pe.wait_ge(w_ready, HALVES * ffn + 2 * j + 1)
                wait(pe, hf_ready, n - 1)
                for k in range(KD):
                    part = slice(k * P, (k + 1) * P)
                    for q, (lhs, rhs) in enumerate(((w_hi, x_hi), (w_hi, x_lo), (w_lo, x_hi))):
                        last = nc.tensor.matmul(h_ps[j % 2][:, 0:tok], lhs[:, j, part], rhs[:, k, 0:tok],
                                                start=(k == 0 and q == 0), stop=(k == KD - 1 and q == 2))
                last.then_inc(h_mm, 1)

            def down(s, ffn, j, kind):
                groups = kind[1] // P
                n = HC * s + j
                pe.wait_ge(w_ready, HALVES * ffn + 2 * j + 2)
                pe.wait_ge(h_ready, n + 1)
                for m in range(groups):
                    if j == 0:
                        wait(pe, out_ready, until(s, kind, M, ME) - (groups - m - 1))
                    part = slice(m * P, (m + 1) * P)
                    for q, (lhs, rhs) in enumerate(((h_hi, w_hi), (h_hi, w_lo), (h_lo, w_hi))):
                        last = nc.tensor.matmul(y_ps[m][:], lhs[:, j % HB, part], rhs[:, j, D:2 * D],
                                                start=(j == 0 and q == 0), stop=(j == HC - 1 and q == 2))
                last.then_inc(y_mm, 1)

            def slot(s, ffn, nxt):
                kind = WIDE if ffn == 0 else NARROW
                for j in range(HC):
                    hidden(s, ffn, j, kind)
                    if j >= 2 and j < HC - 1:
                        down(s, ffn, j - 2, kind)
                    if isinstance(s, int) and s == 0 and j == 6:
                        pe.wait_ge(pick_ready, 1)
                        nc.tensor.matmul(t_ps[0][:, 0:NT], before[:], pick0[:], start=True, stop=True)
                        nc.tensor.matmul(t_ps[0][:, NT:2 * NT], ones[:], pick0[:], start=True, stop=True).then_inc(rank_ps, 1)
                banks = KD // nxt[0]
                transpose(s + 1, nxt, range(0, 2))
                down(s, ffn, HC - 3, kind)
                if banks > 2:
                    transpose(s + 1, nxt, range(2, banks))
                down(s, ffn, HC - 2, kind)
                down(s, ffn, HC - 1, kind)

            transpose(0, WIDE, range(KD))
            slot(0, 0, WIDE)
            pe.wait_ge(t0_ready, 1)
            t0 = read_t0(pe)
            with pe.Fori(1, SHARED - 1) as s:
                slot(s, 0, WIDE)
            slot(SHARED - 1, 0, NARROW)
            pe.wait_ge(acc_step, 2 + 2 * HC)
            pe.wait_ge(xt_lo, until(SHARED + 1, NARROW, KD, KD // 2))
            for e in range(2):
                last = nc.tensor.matmul(t_ps[e][:], ones[:], acc[:, e, :], start=True, stop=True)
            last.then_inc(bias_ps, 1)
            with pe.Fori(SHARED, SHARED + t0) as s:
                slot(s, 1, NARROW)
            with pe.Fori(SHARED + t0, SLOTS) as s:
                slot(s, 2, NARROW)


def kernel(x, cond_1024, L0_cond_weight, L0_ffn_gate_w, L0_ffn_w1, L0_ffn_b1, L0_ffn_w2, L0_ffn_b2,
           L0_ffn_sw1, L0_ffn_sb1, L0_ffn_sw2, L0_ffn_sb2):
    import numpy as np
    import concourse.bacc as bacc
    from concourse.bass_utils import run_bass_kernel_spmd

    def lay(a):
        return np.ascontiguousarray(a)

    x, cond, w_cond, gate = (np.asarray(a) for a in (x, cond_1024, L0_cond_weight, L0_ffn_gate_w))
    w1, b1, w2, b2 = (np.asarray(a) for a in (L0_ffn_w1, L0_ffn_b1, L0_ffn_w2, L0_ffn_b2))
    sw1, sb1, sw2, sb2 = (np.asarray(a) for a in (L0_ffn_sw1, L0_ffn_sb1, L0_ffn_sw2, L0_ffn_sb2))
    rows = x.reshape(N, D)
    up = np.stack([sw1, w1[0], w1[1]]).reshape(3, KD, P, HC, P).transpose(0, 3, 2, 1, 4).reshape(3 * HC, P, D)
    down = np.stack([sw2, w2[0], w2[1]]).reshape(3 * HC, P, D)
    arrays = {
        "x_rows": lay(rows),
        "x_cols": lay(rows.reshape(NT, P, KD, P).transpose(0, 3, 2, 1).reshape(NT, P, D)),
        "cond": lay(cond.reshape(BATCHES, KD, P).transpose(2, 1, 0)),
        "w_cond": lay(w_cond.reshape(KD, P, D).transpose(1, 0, 2)),
        "w_pack": lay(np.stack([up, down], axis=1).reshape(3 * HALVES, P, D)),
        "b1_pack": lay(np.stack([sb1, b1[0], b1[1]]).reshape(3, HC, P).transpose(2, 0, 1)),
        "b2_rows": lay(np.stack([sb2, b2[0], b2[1]])),
        "gate": lay(gate),
    }
    nc = bacc.Bacc("TRN2", target_bir_lowering=False, num_devices=1)
    args = [nc.dram_tensor(n, a.shape, mybir.dt.from_np(a.dtype), kind="ExternalInput").ap() for n, a in arrays.items()]
    out = nc.dram_tensor("out", (N, D), F32, kind="ExternalOutput").ap()
    build(nc, *args, out)
    r = run_bass_kernel_spmd(nc, [arrays], core_ids=[0])
    return r.results[0]["out"].reshape(x.shape)
```

```python
from contextlib import ExitStack

import concourse.bass as bass
from concourse import mybir

F32 = mybir.dt.float32
F32R = mybir.dt.float32r
I32 = mybir.dt.int32
ALU = mybir.AluOpType
ACT = mybir.ActivationFunctionType
AX = mybir.AxisListType

P = 128
N = 4096
D = 512
H = 2048
KD = D // P
HC = H // P
T = 512
TE = 256
M = T // P
ME = TE // P
NT = N // P
WARM_UP = 12
RING = 4
ROUNDS = NT // RING
BATCHES = 2
SHARED = N // T
EXPERT = N // TE + 1
T0_MAX = EXPERT - 1
SLOTS = SHARED + EXPERT
COLS = (EXPERT + 1) * ME
QUADS = HC // 4
HB = 3
HALVES = 2 * HC
STAGE = 4
IDW = 16
PAD = N
EPS = 1e-8
DMA = 16


def wait(eng, sem, value):
    if isinstance(value, int) and value <= 0:
        return
    eng.wait_ge(sem, value)


def wait_apart(eng, sem, value, held):
    if not isinstance(value, int):
        value = eng.snap(value)
        eng.wait_ge(held, 1)
    eng.wait_ge(sem, value)


def block_of(ap, i):
    return ap[i] if isinstance(i, int) else ap[bass.ds(i, 1)].rearrange("a p n -> (a p) n")


def columns(ap, i, n=1):
    return ap[:, i:i + n] if isinstance(i, int) else ap[:, bass.ds(i, n)]


def chunk(ap, j):
    return columns(ap, j).rearrange("p a n -> p (a n)")


def token_rows(ap, n0, n):
    return ap[n0:n0 + n, :] if isinstance(n0, int) else ap[bass.ds(n0, n), :]


def slot_rows(ap, s):
    return token_rows(ap, s * T, T).rearrange("(m p) n -> p m n", p=P)


WIDE = (1, T)
NARROW = (2, TE)


def until(s, kind, shared, expert):
    return shared * s if kind is WIDE else SHARED * shared + (s - SHARED) * expert


def build(nc, x_rows, x_cols, cond, w_cond, w_pack, b1_pack, b2_rows, gate, out):
    xf_dram = nc.dram_tensor("xf_scratch", (N, D), F32).ap()
    part_dram = nc.dram_tensor("partial_scratch", (N, D), F32).ap()
    table_dram = nc.dram_tensor("token_table", (COLS * P, IDW), I32).ap()

    with ExitStack() as ctx:
        def sb(name, shape, dt=F32):
            return ctx.enter_context(nc.sbuf_tensor(name, shape, dt))

        def pb(name):
            return ctx.enter_context(nc.psum_tensor(name, [P, 512], F32))

        def sem(name):
            return ctx.enter_context(nc.semaphore(name))

        w_hi = sb("w_hi", [P, HC, 1024], F32R)
        w_lo = sb("w_lo", [P, HC, 1024], F32R)
        stage = sb("stage", [P, STAGE, D])
        rows = sb("rows", [P, M, D])
        res = sb("res", [P, M, D])
        x_hi = sb("x_hi", [P, KD, T], F32R)
        x_lo = sb("x_lo", [P, KD, T], F32R)
        hf = sb("hf", [P, 2, T])
        h_hi = sb("h_hi", [P, HB, T], F32R)
        h_lo = sb("h_lo", [P, HB, T], F32R)
        scratch = sb("scratch", [P, 4, D])
        bias = sb("bias", [P, 3, D])
        gate_w = sb("gate_w", [P, 2, D])
        ident = sb("ident", [P, P])
        ones = sb("ones", [P, P])
        before = sb("before", [P, P])
        b1 = sb("b1", [P, 3, HC])
        b1_relu = sb("b1_relu", [P, 3, HC])
        cnd = sb("cnd", [P, KD, BATCHES])
        ys = sb("ys", [P, KD, BATCHES])
        ys2 = sb("ys2", [P, KD, BATCHES])
        dcol = sb("dcol", [P, 4, KD * BATCHES])
        score4 = sb("score4", [P, 2, RING])
        score = sb("score", [P, ROUNDS, 2, RING])
        soft = sb("soft", [P, 8, NT])
        pick0 = sb("pick0", [P, NT])
        rank = sb("rank", [P, 2, NT])
        scan = sb("scan", [P, 2, NT])
        place = sb("place", [P, 4, NT])
        order = sb("order", [P, NT])
        steps = sb("steps", [P, EXPERT - 1])
        over = sb("over", [P, EXPERT - 1])
        t0_f = sb("t0_f", [P, 7])
        t0_i = sb("t0_i", [P, 3], I32)
        pos = sb("pos", [P, NT], I32)
        tab = sb("tab", [P, COLS], I32)
        tab_in = sb("tab_in", [P, COLS], I32)
        idx_rows = sb("idx_rows", [P, ME], I32)
        idx_res = sb("idx_res", [P, ME], I32)
        idx_out = sb("idx_out", [P, ME], I32)

        w_raw = rows
        ring = res
        xo = hf
        junk = bias[:, 1, :]
        acc = scratch[:, 0:2, :]
        aux = scratch[:, 2:4, :]
        ids = gate_w[:, :, :].rearrange("p e n -> p (e n)")[:, 0:NT * IDW].bitcast(I32)
        pads = junk[:, 0:COLS * IDW // 2].bitcast(I32)

        y_ps = [pb(f"y_ps{m}") for m in range(M)]
        h_ps = [pb(f"h_ps{i}") for i in range(2)]
        t_ps = [pb(f"t_ps{i}") for i in range(2)]

        const_in = sem("const_in")
        gate_in = sem("gate_in")
        cnd_in = sem("cnd_in")
        w_raw_in = [sem(f"w_raw_in{k}") for k in range(KD)]
        ring_in = [sem(f"ring_in{i}") for i in range(RING)]
        stage_in = [sem(f"stage_in{i}") for i in range(STAGE)]
        rows_in = sem("rows_in")
        res_in = sem("res_in")
        rows_gathered = sem("rows_gathered")
        res_gathered = sem("res_gathered")
        aux_in = sem("aux_in")
        consts_made = sem("consts_made")
        sq_ready = sem("sq_ready")
        v_ready = sem("v_ready")
        v_kept = sem("v_kept")
        d_step = sem("d_step")
        root_ready = sem("root_ready")
        diag_ready = sem("diag_ready")
        d_ready = sem("d_ready")
        wc0_scaled = sem("wc0_scaled")
        wc0_hi = sem("wc0_hi")
        wc0_ready = sem("wc0_ready")
        wc1_scaled = sem("wc1_scaled")
        wc1_hi = sem("wc1_hi")
        wc1_ready = sem("wc1_ready")
        tile_hi = sem("tile_hi")
        tile_lo = sem("tile_lo")
        tile_mm = sem("tile_mm")
        xf_ready = sem("xf_ready")
        xf_out = [sem(f"xf_out{i}") for i in range(2)]
        gate_half = sem("gate_half")
        gate_done = sem("gate_done")
        score_kept = sem("score_kept")
        route = sem("route")
        soft_in = sem("soft_in")
        soft_exp = sem("soft_exp")
        pick_ready = sem("pick_ready")
        rank_ps = sem("rank_ps")
        t0_ready = sem("t0_ready")
        pos_ready = sem("pos_ready")
        fills_made = sem("fills_made")
        pads_out = sem("pads_out")
        ids_made = sem("ids_made")
        ids_out = sem("ids_out")
        tab_dma = sem("tab_dma")
        tab_ready = sem("tab_ready")
        w_hi_ready = sem("w_hi_ready")
        w_ready = sem("w_ready")
        xt_ps = sem("xt_ps")
        xt_hi = sem("xt_hi")
        xt_lo = sem("xt_lo")
        h_mm = sem("h_mm")
        hf_ready = sem("hf_ready")
        hh_ready = sem("hh_ready")
        h_ready = sem("h_ready")
        y_mm = sem("y_mm")
        res_biased = sem("res_biased")
        out_ready = sem("out_ready")
        part_out = sem("part_out")
        scattered = sem("scattered")
        flat_ready = sem("flat_ready")
        back_ps = sem("back_ps")
        acc_step = sem("acc_step")
        bias_ps = sem("bias_ps")
        bias_step = sem("bias_step")

        def read_split(eng):
            eng.wait_ge(t0_ready, 1)
            t0, full0, full1 = (eng.value_load(t0_i[0:1, i:i + 1], min_val=1, max_val=T0_MAX) for i in range(3))
            return t0, eng.snap(full0 + SHARED), eng.snap(t0 + full1 + SHARED)

        def bank(s, f):
            return (t_ps + y_ps[2:])[f] if is_number(s, 0) else t_ps[f % 2]

        def is_number(s, number):
            return isinstance(s, int) and s == number

        def group_of_slot_0(m):
            return bank(0, m)[:].rearrange("p (k n) -> p k n", k=KD), slice(m * P, (m + 1) * P)

        block = ctx.enter_context(nc.Block())

        @block.sync
        def _(sp):
            sp.dma_start(cnd[:], cond).then_inc(cnd_in, DMA)
            for k in range(KD):
                sp.dma_start(w_raw[:, k, :], w_cond[:, k, :]).then_inc(w_raw_in[k], DMA)
            for i in range(RING):
                sp.dma_start(ring[:, i, :], x_cols[i]).then_inc(ring_in[i], DMA)
            sp.dma_start(gate_w[:], gate.partition_broadcast(P)).then_inc(gate_in, DMA)
            sp.dma_start(b1[:], b1_pack).then_inc(const_in, DMA)
            sp.dma_start(bias[:, 0, :], b2_rows[0].partition_broadcast(P)).then_inc(const_in, DMA)
            for i in range(STAGE):
                sp.dma_start(stage[:, i, :], w_pack[i]).then_inc(stage_in[i], DMA)

            def weight_halves(u):
                for i in range(STAGE):
                    sp.wait_ge(w_ready, STAGE * (u - 1) + i + 1)
                    sp.dma_start(stage[:, i, :], block_of(w_pack, STAGE * u + i)).then_inc(stage_in[i], DMA)

            def tiles_round(t, more):
                for i in range(RING):
                    c = t * RING + i
                    sp.wait_ge(xf_ready, c + 1)
                    sp.dma_start(token_rows(xf_dram, c * P, P), xo[:, i % 2, :]).then_inc(xf_out[i % 2], DMA)
                    if more:
                        sp.wait_ge(tile_lo, c + 1)
                        sp.dma_start(ring[:, i, :], block_of(x_cols, c + RING)).then_inc(ring_in[i], DMA)

            with sp.Fori(0, ROUNDS // 2) as t:
                tiles_round(t, True)
            for i in range(2):
                sp.wait_ge(xf_out[i], 2 * DMA)
            sp.wait_ge(wc1_ready, KD)
            sp.dma_start(rows[:], slot_rows(xf_dram, 0)).then_inc(rows_in, DMA)
            with sp.Fori(ROUNDS // 2, ROUNDS - 1) as t:
                tiles_round(t, True)
            tiles_round(ROUNDS - 1, False)

            weight_halves(1)
            sp.wait_ge(tile_lo, NT)
            sp.dma_start(res[:], slot_rows(x_rows, 0)).then_inc(res_in, DMA)

            w2_pair = w_pack.rearrange("(f j h) p n -> h j p f n", f=3, h=2)[1, :, :, 1:3, :]

            def aux_load(j):
                sp.wait_ge(acc_step, 2 + 2 * j)
                src = w2_pair[j] if isinstance(j, int) else w2_pair[bass.ds(j, 1)].rearrange("a p f n -> (a p) f n")
                sp.dma_start(aux, src).then_inc(aux_in, DMA)

            def next_rows(s):
                sp.wait_ge(xt_ps, KD * (s + 1))
                sp.dma_start(rows[:], slot_rows(xf_dram, s + 1)).then_inc(rows_in, DMA)

            def store(s):
                for m in range(M):
                    sp.wait_ge(out_ready, M * s + m + 1)
                    sp.dma_start(token_rows(part_dram, (M * s + m) * P, P), res[:, m, :]).then_inc(part_out, DMA)

            def next_res(s):
                sp.wait_ge(part_out, M * DMA * (s + 1))
                sp.dma_start(res[:], slot_rows(x_rows, s + 1)).then_inc(res_in, DMA)

            aux_load(0)
            for u in range(2, 4):
                weight_halves(u)
            aux_load(1)
            for i in range(2):
                sp.wait_ge(xf_out[i], DMA * NT // 2)
            next_rows(0)
            for u in range(4, HALVES // STAGE + 1):
                weight_halves(u)
            aux_load(2)
            store(0)
            next_res(0)
            with sp.Fori(1, SHARED - 1) as s:
                next_rows(s)
                aux_load(2 * s + 1)
                aux_load(2 * s + 2)
                store(s)
                next_res(s)
            aux_load(HC - 1)
            sp.wait_ge(acc_step, 2 + 2 * HC)
            for e in range(2):
                sp.dma_start(aux[:, e, :], b2_rows[1 + e].partition_broadcast(P)).then_inc(const_in, DMA)
            weight_halves(HALVES // STAGE + 1)
            store(SHARED - 1)
            with sp.Fori(HALVES // STAGE + 2, 3 * HALVES // STAGE) as u:
                weight_halves(u)

        @block.gpsimd
        def _(pool):
            pool.memset(ident[:], 0.0).then_inc(fills_made, 1)
            pool.memset(ones[:], 1.0).then_inc(fills_made, 1)
            pool.memset(pads, PAD).then_inc(fills_made, 1)
            pool.wait_ge(fills_made, 3)
            pool.affine_select(out=ident[:], in_=ident[:], compare_op=ALU.not_equal, fill=1.0, base=0,
                               pattern=[[-1, P]], channel_multiplier=1).then_inc(consts_made, 1)
            pool.affine_select(out=before[:], in_=ones[:], compare_op=ALU.is_gt, fill=0.0, base=0,
                               pattern=[[1, P]], channel_multiplier=-1).then_inc(consts_made, 1)
            pool.iota(order[:], [[P, NT]], base=0, channel_multiplier=1,
                      allow_small_or_imprecise_dtypes=True).then_inc(consts_made, 1)
            pool.iota(steps[:], [[TE, EXPERT - 1]], base=0, channel_multiplier=0,
                      allow_small_or_imprecise_dtypes=True).then_inc(consts_made, 1)
            half = COLS * IDW // 2
            table_p = table_dram.rearrange("(p c) w -> p (c w)", p=P)
            for i in range(2):
                pool.dma_start(table_p[:, i * half:(i + 1) * half], pads).then_inc(pads_out, DMA)

            pool.wait_ge(gate_done, NT)
            pool.iota(ids, [[P, NT], [0, IDW]], base=0, channel_multiplier=1).then_inc(ids_made, 1)
            pool.wait_ge(ids_made, 1)
            pool.wait_ge(pads_out, 2 * DMA)
            pool.wait_ge(pos_ready, 1)
            for c in range(NT):
                pool.indirect_dma_start(table_dram, bass.IndirectOffsetOnAxis(pos[:, c:c + 1], 0),
                                        ids[:, c * IDW:(c + 1) * IDW], None).then_inc(ids_out, DMA)
            pool.wait_ge(ids_out, NT * DMA)
            with nc.allow_non_contiguous_dma(reason="one number per 64-byte row"):
                pool.dma_start(tab[:], table_dram.rearrange("(c p) w -> p c w", p=P)[:, :, 0]).then_inc(tab_dma, DMA)
            pool.wait_ge(tab_dma, DMA)
            pool.tensor_scalar(tab_in[:], tab[:], N - 1, None, ALU.min).then_inc(tab_ready, 1)
            pool.wait_ge(tab_ready, 1)

            def numbers(dst, table, s):
                pool.tensor_copy(dst[:], columns(table, (s - SHARED) * ME, ME))
                pool.drain()

            def gather_rows(s):
                wait_apart(pool, xt_ps, until(s, NARROW, KD, KD // 2), tab_ready)
                numbers(idx_rows, tab_in, s)
                for m in range(ME):
                    pool.indirect_dma_start(rows[:, m, :], None, xf_dram,
                                            bass.IndirectOffsetOnAxis(idx_rows[:, m:m + 1], 0)).then_inc(rows_gathered, DMA)

            def gather_res(s):
                if isinstance(s, int):
                    pool.wait_ge(part_out, M * DMA * SHARED)
                else:
                    wait_apart(pool, scattered, ME * DMA * (s - SHARED), tab_ready)
                numbers(idx_res, tab_in, s)
                for m in range(ME):
                    pool.indirect_dma_start(res[:, m, :], None, part_dram,
                                            bass.IndirectOffsetOnAxis(idx_res[:, m:m + 1], 0)).then_inc(res_gathered, DMA)

            def scatter(m):
                pool.indirect_dma_start(out, bass.IndirectOffsetOnAxis(idx_out[:, m:m + 1], 0), res[:, m, :], None,
                                        bounds_check=N - 1, oob_is_err=False).then_inc(scattered, DMA)

            def scatter_out(s):
                wait_apart(pool, out_ready, until(s + 1, NARROW, M, ME), tab_ready)
                numbers(idx_out, tab, s)
                for m in range(ME):
                    scatter(m)

            for i in range(2):
                pool.wait_ge(xf_out[i], DMA * NT // 2)
            gather_rows(SHARED)
            gather_rows(SHARED + 1)
            gather_res(SHARED)
            with pool.Fori(SHARED + 1, SLOTS) as s:
                scatter_out(s - 1)
                gather_rows(s + 1)
                gather_res(s)
            numbers(idx_out, tab, SLOTS - 1)
            for m in range(ME):
                pool.wait_ge(out_ready, until(SLOTS - 1, NARROW, M, ME) + m + 1)
                scatter(m)
            pool.wait_ge(scattered, ME * DMA * EXPERT)
            pool.wait_ge(rows_gathered, ME * DMA * (EXPERT + 1))

        @block.scalar
        def _(act):
            def split_hi(t, i):
                act.wait_ge(ring_in[i], DMA * (t + 1))
                wait(act, tile_mm, RING * t + i + 1 - RING)
                nc.scalar.copy(x_hi[:, :, i * P:(i + 1) * P],
                               ring[:, i, :].rearrange("p (k n) -> p k n", k=KD)).then_inc(tile_hi, 1)

            def take_xf(t, i):
                c = RING * t + i
                act.wait_ge(tile_mm, c + 1)
                wait(act, gate_done, c - 1)
                wait(act, xf_out[i % 2], DMA * (2 * t + i // 2))
                nc.scalar.copy(xo[:, i % 2, :], h_ps[i % 2][:]).then_inc(xf_ready, 1)

            def wc1_part(k):
                act.wait_ge(wc1_scaled, k + 1)
                nc.scalar.copy(chunk(w_hi, 8 + k)[:, D:2 * D], chunk(scratch, k)).then_inc(wc1_hi, 1)

            def weights_hi(ffn, j):
                for half in range(2):
                    h = HALVES * ffn + 2 * j + half
                    act.wait_ge(stage_in[h % STAGE], DMA * (h // STAGE + 1))
                    nc.scalar.copy(w_hi[:, j, half * D:(half + 1) * D], stage[:, h % STAGE, :]).then_inc(w_hi_ready, 1)

            def group_hi(m):
                features, part = group_of_slot_0(m)
                act.wait_ge(xt_ps, m + 1)
                act.wait_ge(tile_mm, NT - M + m + 1)
                nc.scalar.copy(x_hi[:, :, part], features).then_inc(xt_hi, 1)

            def tiles_round(t, last, wc1):
                for i in range(RING):
                    if i < 2:
                        if not is_number(t, 0):
                            split_hi(t, i + 2)
                    elif not last:
                        split_hi(t + 1, i - 2)
                    if last and i < 2:
                        weights_hi(0, i)
                    if last and i == RING - 1:
                        group_hi(i)
                    take_xf(t, i)
                    if wc1 and i == 0:
                        wc1_part(t)
                    if last and i < RING - 1:
                        group_hi(i)

            act.wait_ge(d_step, 2)
            nc.scalar.activation(dcol[:, 2, :], dcol[:, 1, :], ACT.Sqrt).then_inc(root_ready, 1)
            split_hi(0, 0)
            split_hi(0, 1)
            for k in range(KD):
                act.wait_ge(wc0_scaled, k + 1)
                nc.scalar.copy(w_hi[:, 12 + k, D:2 * D], scratch[:, k, :]).then_inc(wc0_hi, 1)
            split_hi(0, 2)
            split_hi(0, 3)
            tiles_round(0, False, True)
            with act.Fori(1, ROUNDS // 2) as t:
                tiles_round(t, False, True)
            with act.Fori(ROUNDS // 2, ROUNDS - 1) as t:
                tiles_round(t, False, False)
            tiles_round(ROUNDS - 1, True, False)

            def transposed(s, kind):
                per_bank, tok = kind
                for f in range(KD // per_bank):
                    act.wait_ge(xt_ps, until(s, kind, KD, KD // 2) + f + 1)
                    nc.scalar.copy(x_hi[:, f * per_bank:(f + 1) * per_bank, 0:tok],
                                   bank(s, f)[:].rearrange("p (k n) -> p k n", k=per_bank)).then_inc(xt_hi, 1)

            def slot(s, ffn, first, nxt):
                tok = T if ffn == 0 else TE
                for j in range(HC):
                    n = HC * s + j
                    if first and ffn > 0 and j == 0:
                        weights_hi(ffn, 2)
                    act.wait_ge(h_mm, n + 1)
                    wait(act, h_ready, n - 1)
                    nc.scalar.activation(hf[:, j % 2, 0:tok], h_ps[j % 2][:, 0:tok], ACT.Relu,
                                         bias=b1[:, ffn, j:j + 1]).then_inc(hf_ready, 1)
                    if first and j + 2 < HC and (ffn == 0 or j > 0):
                        if j == 0:
                            act.wait_ge(tile_mm, NT)
                        if j == 1:
                            wait(act, y_mm, HC * s)
                        weights_hi(ffn, j + 2)
                    if isinstance(s, int) and s == 0 and j == 2:
                        act.wait_ge(soft_in, 3)
                        nc.scalar.activation(soft[:, 3:5, :], soft[:, 1:3, :], ACT.Exp).then_inc(soft_exp, 1)
                transposed(s + 1, nxt)

            def short_slot(s, ffn):

                def flat(u):
                    act.wait_ge(h_mm, HC * s + 4 * (u + 1))
                    act.wait_ge(h_ready, HC * s + 4 * max(u - 1, 0))
                    nc.scalar.copy(hf[:, u % 2, :], h_ps[u % 2][:]).then_inc(flat_ready, 1)

                flat(0)
                for u in range(QUADS):
                    if u + 1 < QUADS:
                        flat(u + 1)
                    act.wait_ge(back_ps, u + 1)
                    for i in range(4):
                        part = slice(i * P, (i + 1) * P)
                        nc.scalar.activation(hf[:, u % 2, part], t_ps[u % 2][:, part], ACT.Relu,
                                             bias=b1[:, ffn, 4 * u + i:4 * u + i + 1]).then_inc(hf_ready, 1)
                transposed(s + 1, NARROW)

            def change(s, ffn):
                act.wait_ge(y_mm, HC * (s - 1) + 3)
                for j in range(2):
                    weights_hi(ffn, j)

            act.wait_ge(gate_done, NT)
            for i in range(2):
                act.wait_ge(xf_out[i], DMA * NT // 2)
            act.wait_ge(const_in, 2 * DMA)
            slot(0, 0, True, WIDE)
            t0, end0, end1 = read_split(act)
            with act.Fori(1, SHARED - 1) as s:
                slot(s, 0, False, WIDE)
            slot(SHARED - 1, 0, False, NARROW)
            change(SHARED, 1)
            slot(SHARED, 1, True, NARROW)
            with act.If(end0 > SHARED + 1):
                with act.Fori(SHARED + 1, end0) as s:
                    slot(s, 1, False, NARROW)
            s1 = act.snap(t0 + SHARED)
            with act.If(end0 < s1):
                short_slot(end0, 1)
            change(s1, 2)
            slot(s1, 2, True, NARROW)
            with act.If(end1 > s1 + 1):
                with act.Fori(s1 + 1, end1) as s:
                    slot(s, 2, False, NARROW)
            with act.If(end1 < SLOTS):
                short_slot(end1, 2)

        @block.vector
        def _(dve):
            def split_lo(t, i):
                dve.wait_ge(tile_hi, RING * t + i + 1)
                x_part = slice(i * P, (i + 1) * P)
                nc.vector.tensor_tensor(x_lo[:, :, x_part], ring[:, i, :].rearrange("p (k n) -> p k n", k=KD),
                                        x_hi[:, :, x_part].bitcast(F32), ALU.subtract).then_inc(tile_lo, 1)

            dve.wait_ge(cnd_in, DMA)
            nc.vector.tensor_scalar(ys[:], cnd[:], float(D) ** -0.5, None, ALU.mult).then_inc(d_step, 1)
            dve.wait_ge(d_step, 1)
            nc.vector.tensor_tensor(ys2[:], ys[:], ys[:], ALU.mult).then_inc(sq_ready, 1)
            for k in range(KD):
                dve.wait_ge(w_raw_in[k], DMA)
                nc.vector.tensor_tensor(scratch[:, k, :], w_raw[:, k, :], w_raw[:, k, :], ALU.mult).then_inc(sq_ready, 1)
            for o in range(KD):
                dve.wait_ge(v_ready, o + 1)
                nc.vector.tensor_scalar(dcol[:, 0, o * BATCHES:(o + 1) * BATCHES], bank(0, o)[:, 0:BATCHES], EPS, None,
                                        ALU.add).then_inc(v_kept, 1)
            dve.wait_ge(v_kept, KD)
            nc.vector.reciprocal(dcol[:, 1, :], dcol[:, 0, :]).then_inc(d_step, 1)
            dve.wait_ge(root_ready, 1)
            nc.vector.tensor_tensor(dcol[:, 3, :], dcol[:, 2, :], dcol[:, 2, :], ALU.mult).then_inc(d_step, 1)
            dve.wait_ge(d_step, 3)
            nc.vector.tensor_tensor(dcol[:, 3, :], dcol[:, 3, :], dcol[:, 0, :], ALU.mult).then_inc(d_step, 1)
            dve.wait_ge(d_step, 4)
            nc.vector.tensor_scalar(dcol[:, 3, :], dcol[:, 3, :], -0.5, 1.5, ALU.mult, ALU.add).then_inc(d_step, 1)
            dve.wait_ge(d_step, 5)
            nc.vector.tensor_tensor(dcol[:, 2, :], dcol[:, 2, :], dcol[:, 3, :], ALU.mult).then_inc(d_step, 1)
            dve.wait_ge(d_step, 6)
            dve.wait_ge(consts_made, 1)
            d_ob = dcol[:, 2, :].rearrange("p (o b) -> p o b", b=BATCHES)

            def diagonals(b):
                nc.vector.tensor_tensor(hf[:, b, :].rearrange("p (o n) -> p o n", o=KD),
                                        ident[:].unsqueeze(1).broadcast_to([P, KD, P]),
                                        d_ob[:, :, b:b + 1].broadcast_to([P, KD, P]), ALU.mult).then_inc(diag_ready, 1)

            def wc0_low(k):
                dve.wait_ge(wc0_hi, k + 1)
                nc.vector.tensor_tensor(w_lo[:, 12 + k, D:2 * D], scratch[:, k, :], w_hi[:, 12 + k, D:2 * D].bitcast(F32),
                                        ALU.subtract).then_inc(wc0_ready, 1)

            diagonals(0)
            diagonals(1)
            split_lo(0, 0)
            split_lo(0, 1)
            dve.wait_ge(d_ready, 1)
            for k in range(KD):
                nc.vector.scalar_tensor_tensor(out=scratch[:, k, :], in0=w_raw[:, k, :], scalar=ys[:, k, 0:1],
                                               in1=y_ps[0][:], op0=ALU.mult, op1=ALU.mult).then_inc(wc0_scaled, 1)
                if k > 0:
                    wc0_low(k - 1)
            wc0_low(KD - 1)
            split_lo(0, 2)
            split_lo(0, 3)

            dve.wait_ge(pads_out, 2 * DMA)
            dve.wait_ge(gate_in, DMA)

            def wc1_part(k):
                nc.vector.scalar_tensor_tensor(out=chunk(scratch, k), in0=chunk(w_raw, k),
                                               scalar=columns(ys[:, :, 1], k), in1=y_ps[1][:], op0=ALU.mult,
                                               op1=ALU.mult).then_inc(wc1_scaled, 1)

            def wc1_rest(k):
                dve.wait_ge(wc1_hi, k + 1)
                nc.vector.tensor_tensor(chunk(w_lo, 8 + k)[:, D:2 * D], chunk(scratch, k),
                                        chunk(w_hi, 8 + k)[:, D:2 * D].bitcast(F32),
                                        ALU.subtract).then_inc(wc1_ready, 1)

            def weights_lo(ffn, j, halves=(0, 1)):
                for half in halves:
                    h = HALVES * ffn + 2 * j + half
                    part = slice(half * D, (half + 1) * D)
                    dve.wait_ge(w_hi_ready, h + 1)
                    nc.vector.tensor_tensor(w_lo[:, j, part], stage[:, h % STAGE, :], w_hi[:, j, part].bitcast(F32),
                                            ALU.subtract).then_inc(w_ready, 1)

            def gate_scores(t, i):
                c = RING * t + i
                dve.wait_ge(xf_ready, c + 1)
                if i == 0:
                    wait(dve, score_kept, t)
                for e in range(2):
                    wait(dve, gate_half if e else gate_done, c + e)
                    nc.vector.tensor_tensor_reduce(out=junk, in0=xo[:, i % 2, :], in1=gate_w[:, e, :], scale=1.0,
                                                   scalar=0.0, op0=ALU.mult, op1=ALU.add,
                                                   accum_out=score4[:, e, i:i + 1]).then_inc(gate_done if e else gate_half, 1)
                if i == RING - 1:
                    dve.wait_ge(gate_done, c + 1)
                    nc.vector.tensor_copy(columns(score, t).rearrange("p a e i -> p (a e) i"), score4[:]).then_inc(score_kept, 1)

            def group_lo(m):
                features, part = group_of_slot_0(m)
                dve.wait_ge(xt_hi, m + 1)
                nc.vector.tensor_tensor(x_lo[:, :, part], features, x_hi[:, :, part].bitcast(F32),
                                        ALU.subtract).then_inc(xt_lo, 1)

            def tiles_round(t, last, wc1):
                for i in range(RING):
                    if i < 2:
                        if not is_number(t, 0):
                            split_lo(t, i + 2)
                    elif not last:
                        split_lo(t + 1, i - 2)
                    if wc1 and i == 1:
                        wc1_rest(t)
                    if wc1 and i == 3 and not (isinstance(t, int) and t == ROUNDS // 2 - 1):
                        wc1_part(t + 1)
                    if last and i == 0:
                        weights_lo(0, 0, (0,))
                    if last and i == RING - 1:
                        group_lo(i)
                        weights_lo(0, 0, (1,))
                        weights_lo(0, 1, (0,))
                    gate_scores(t, i)
                    if last and i < RING - 1:
                        group_lo(i)

            dve.wait_ge(d_ready, 2)
            wc1_part(0)
            tiles_round(0, False, True)
            with dve.Fori(1, ROUNDS // 2 - 1) as t:
                tiles_round(t, False, True)
            tiles_round(ROUNDS // 2 - 1, False, True)
            with dve.Fori(ROUNDS // 2, ROUNDS - 1) as t:
                tiles_round(t, False, False)
            tiles_round(ROUNDS - 1, True, False)
            weights_lo(0, 1, (1,))

            def transposed(s, kind):
                per_bank, tok = kind
                for f in range(KD // per_bank):
                    ks = slice(f * per_bank, (f + 1) * per_bank)
                    dve.wait_ge(xt_hi, until(s, kind, KD, KD // 2) + f + 1)
                    nc.vector.tensor_tensor(x_lo[:, ks, 0:tok], bank(s, f)[:].rearrange("p (k n) -> p k n", k=per_bank),
                                            x_hi[:, ks, 0:tok].bitcast(F32), ALU.subtract).then_inc(xt_lo, 1)

            r = [0]

            def step(ins):
                r[0] += 1
                ins.then_inc(route, 1)
                dve.wait_ge(route, r[0])

            def softmax_start():
                def cols(ap):
                    return ap.rearrange("p (t i) -> p t i", i=RING)

                g0, g1 = score[:, :, 0, :], score[:, :, 1, :]
                dve.wait_ge(score_kept, ROUNDS)
                nc.vector.tensor_tensor(cols(soft[:, 0, :]), g0, g1, ALU.max).then_inc(soft_in, 1)
                dve.wait_ge(soft_in, 1)
                nc.vector.tensor_tensor(cols(soft[:, 1, :]), g0, cols(soft[:, 0, :]), ALU.subtract).then_inc(soft_in, 1)
                nc.vector.tensor_tensor(cols(soft[:, 2, :]), g1, cols(soft[:, 0, :]), ALU.subtract).then_inc(soft_in, 1)

            def choose():
                dve.wait_ge(soft_exp, 1)
                step(nc.vector.tensor_tensor(soft[:, 5, :], soft[:, 3, :], soft[:, 4, :], ALU.add))
                step(nc.vector.reciprocal(soft[:, 6, :], soft[:, 5, :]))
                step(nc.vector.tensor_tensor(soft[:, 0, :], soft[:, 3, :], soft[:, 6, :], ALU.mult))
                step(nc.vector.tensor_tensor(soft[:, 7, :], soft[:, 4, :], soft[:, 6, :], ALU.mult))
                nc.vector.tensor_tensor(pick0[:], soft[:, 0, :], soft[:, 7, :], ALU.is_ge).then_inc(pick_ready, 1)

            def count():
                dve.wait_ge(rank_ps, 1)
                step(nc.vector.tensor_copy(rank[:], t_ps[0][:, 0:2 * NT].rearrange("p (a c) -> p a c", a=2)))
                step(nc.vector.tensor_copy(scan[:, 0, :], rank[:, 1, :]))
                a = 0
                for sh in (1, 2, 4, 8, 16):
                    r[0] += 1
                    nc.vector.tensor_copy(scan[:, 1 - a, 0:sh], scan[:, a, 0:sh]).then_inc(route, 1)
                    step(nc.vector.tensor_tensor(scan[:, 1 - a, sh:NT], scan[:, a, sh:NT], scan[:, a, 0:NT - sh], ALU.add))
                    a = 1 - a

            def places():
                total = scan[:, 1, NT - 1:NT]
                step(nc.vector.tensor_scalar(over[:, 1:T0_MAX], steps[:, 1:T0_MAX], total, None, ALU.is_lt))
                step(nc.vector.reduce_sum(t0_f[:, 0:1], over[:, 1:T0_MAX], AX.X))
                step(nc.vector.tensor_scalar(t0_f[:, 1:2], t0_f[:, 0:1], 1.0, None, ALU.add))
                step(nc.vector.tensor_scalar(over[:, 0:1], t0_f[:, 1:2], float(TE), None, ALU.mult))
                step(nc.vector.tensor_scalar(t0_f[:, 4:5], total, float(P), over[:, 0:1], ALU.add, ALU.is_le))
                step(nc.vector.tensor_scalar(t0_f[:, 5:6], total, float(P), over[:, 0:1], ALU.add, ALU.is_gt))
                step(nc.vector.tensor_tensor(t0_f[:, 2:3], t0_f[:, 1:2], t0_f[:, 4:5], ALU.subtract))
                step(nc.vector.tensor_scalar(t0_f[:, 2:3], t0_f[:, 2:3], 1.0, None, ALU.max))
                step(nc.vector.tensor_scalar(t0_f[:, 6:7], t0_f[:, 1:2], -1.0, float(EXPERT), ALU.mult, ALU.add))
                step(nc.vector.tensor_tensor(t0_f[:, 3:4], t0_f[:, 6:7], t0_f[:, 5:6], ALU.subtract))
                step(nc.vector.tensor_scalar(t0_f[:, 3:4], t0_f[:, 3:4], 1.0, None, ALU.max))
                nc.vector.tensor_copy(t0_i[:], t0_f[:, 1:4]).then_inc(t0_ready, 1)
                step(nc.vector.tensor_tensor(place[:, 0, :], scan[:, 1, :], rank[:, 1, :], ALU.subtract))
                step(nc.vector.tensor_tensor(place[:, 1, :], place[:, 0, :], rank[:, 0, :], ALU.add))
                step(nc.vector.tensor_tensor(place[:, 2, :], order[:], place[:, 1, :], ALU.subtract))
                step(nc.vector.tensor_scalar(place[:, 2, :], place[:, 2, :], over[:, 0:1], None, ALU.add))
                step(nc.vector.tensor_tensor(place[:, 3, :], place[:, 1, :], place[:, 2, :], ALU.subtract))
                step(nc.vector.tensor_tensor(place[:, 3, :], place[:, 3, :], pick0[:], ALU.mult))
                nc.vector.tensor_tensor(pos[:], place[:, 2, :], place[:, 3, :], ALU.add).then_inc(pos_ready, 1)

            def constant_rows(s, which):
                ch = 2 * s + which
                dve.wait_ge(aux_in, DMA * (ch + 1))
                dve.wait_ge(acc_step, 2 + 2 * ch)
                for e in range(2):
                    nc.vector.scalar_tensor_tensor(out=acc[:, e, :], in0=aux[:, e, :],
                                                   scalar=columns(b1_relu[:, 1 + e, :], ch), in1=acc[:, e, :],
                                                   op0=ALU.mult, op1=ALU.add).then_inc(acc_step, 1)

            def add_bias(s, ffn, m):
                if ffn == 0:
                    dve.wait_ge(res_in, DMA * (s + 1))
                else:
                    dve.wait_ge(res_gathered, ME * DMA * (s - SHARED + 1))
                nc.vector.tensor_tensor(res[:, m, :], res[:, m, :], bias[:, ffn, :], ALU.add).then_inc(res_biased, 1)

            def finish(s, kind):
                for m in range(kind[1] // P):
                    dve.wait_ge(y_mm, HC * (s + 1))
                    dve.wait_ge(res_biased, until(s, kind, M, ME) + m + 1)
                    nc.vector.tensor_tensor(res[:, m, :], y_ps[m][:], res[:, m, :], ALU.add).then_inc(out_ready, 1)

            def expert_rows():
                dve.wait_ge(bias_ps, 1)
                dve.wait_ge(const_in, 4 * DMA)
                nc.vector.tensor_tensor(bias[:, 1, :], aux[:, 0, :], aux[:, 1, :], ALU.add).then_inc(bias_step, 1)
                dve.wait_ge(bias_step, 1)
                for e in (1, 0):
                    nc.vector.tensor_tensor(bias[:, 1 + e, :], t_ps[1 - e][:], bias[:, 1, :], ALU.add).then_inc(bias_step, 1)
                dve.wait_ge(bias_step, 3)

            def slot(s, ffn, first, nxt):
                tok, groups = (T, M) if ffn == 0 else (TE, ME)
                at_start = isinstance(s, int) and s == 0
                if not at_start:
                    finish(s - 1, WIDE if ffn == 0 or isinstance(s, int) else NARROW)
                for j in range(HC):
                    n = HC * s + j
                    buf = j % HB
                    if first and ffn > 0 and j == 0:
                        weights_lo(ffn, 2)
                    dve.wait_ge(hf_ready, n + 1)
                    wait(dve, y_mm, n - HB + 1 if j >= HB else HC * s)
                    nc.vector.tensor_copy(h_hi[:, buf, 0:tok], hf[:, j % 2, 0:tok]).then_inc(hh_ready, 1)
                    dve.wait_ge(hh_ready, n + 1)
                    nc.vector.tensor_tensor(h_lo[:, buf, 0:tok], hf[:, j % 2, 0:tok], h_hi[:, buf, 0:tok].bitcast(F32),
                                            ALU.subtract).then_inc(h_ready, 1)
                    if first and j + 2 < HC and (ffn == 0 or j > 0):
                        weights_lo(ffn, j + 2)
                    if ffn == 0 and j in (3, 10):
                        constant_rows(s, 0 if j == 3 else 1)
                    if j in (8, 12, 13, 14)[:groups]:
                        m = (8, 12, 13, 14).index(j)
                        add_bias(s, ffn, m)
                    if at_start and j == 0:
                        nc.vector.memset(acc, 0.0).then_inc(acc_step, 1)
                        dve.wait_ge(const_in, 2 * DMA)
                        nc.vector.tensor_scalar(b1_relu[:], b1[:], 0.0, None, ALU.max).then_inc(acc_step, 1)
                    if at_start and j == 1:
                        softmax_start()
                    if at_start and j == 4:
                        choose()
                    if at_start and j == 7:
                        count()
                    if at_start and j == 9:
                        places()
                    if isinstance(s, int) and s == SHARED and j == 4:
                        expert_rows()
                transposed(s + 1, nxt)

            def short_slot(s, ffn):
                finish(s - 1, NARROW)
                for u in range(QUADS):
                    n = HC * s + 4 * u
                    dve.wait_ge(hf_ready, n + 4)
                    dve.wait_ge(y_mm, n - 4 * (HB - 1) if u >= HB else HC * s)
                    nc.vector.tensor_copy(h_hi[:, u % HB, :], hf[:, u % 2, :]).then_inc(hh_ready, 4)
                    dve.wait_ge(hh_ready, n + 4)
                    nc.vector.tensor_tensor(h_lo[:, u % HB, :], hf[:, u % 2, :], h_hi[:, u % HB, :].bitcast(F32),
                                            ALU.subtract).then_inc(h_ready, 4)
                    if u >= QUADS - ME:
                        add_bias(s, ffn, u - (QUADS - ME))
                transposed(s + 1, NARROW)

            slot(0, 0, True, WIDE)
            t0, end0, end1 = read_split(dve)
            with dve.Fori(1, SHARED - 1) as s:
                slot(s, 0, False, WIDE)
            slot(SHARED - 1, 0, False, NARROW)

            def change(ffn):
                for j in range(2):
                    weights_lo(ffn, j)

            change(1)
            slot(SHARED, 1, True, NARROW)
            with dve.If(end0 > SHARED + 1):
                with dve.Fori(SHARED + 1, end0) as s:
                    slot(s, 1, False, NARROW)
            s1 = dve.snap(t0 + SHARED)
            with dve.If(end0 < s1):
                short_slot(end0, 1)
            change(2)
            slot(s1, 2, True, NARROW)
            with dve.If(end1 > s1 + 1):
                with dve.Fori(s1 + 1, end1) as s:
                    slot(s, 2, False, NARROW)
            with dve.If(end1 < SLOTS):
                short_slot(end1, 2)
            finish(SLOTS - 1, NARROW)

        @block.tensor
        def _(pe):
            pe.wait_ge(fills_made, 2)
            for _ in range(WARM_UP):
                nc.tensor.matmul(h_ps[0][:, 0:P], ones[:], ones[:], start=True, stop=True)
            for k in range(KD):
                pe.wait_ge(sq_ready, k + 2)
                for o in range(KD):
                    last = nc.tensor.matmul(bank(0, o)[:, 0:BATCHES], scratch[:, k, o * P:(o + 1) * P],
                                            ys2[:, k, :], start=(k == 0), stop=(k == KD - 1))
                    if k == KD - 1:
                        last.then_inc(v_ready, 1)
            pe.wait_ge(consts_made, 4)

            def spread_d(b):
                pe.wait_ge(diag_ready, b + 1)
                nc.tensor.matmul(y_ps[b][:], ones[:], hf[:, b, :], start=True, stop=True).then_inc(d_ready, 1)

            for b in range(BATCHES):
                spread_d(b)

            def project_chunk(i, b, k, passes=range(3)):
                part = slice(i * P, (i + 1) * P)
                w = 12 - 4 * b + k
                for q in passes:
                    lhs, rhs = ((x_hi, w_hi), (x_lo, w_hi), (x_hi, w_lo))[q]
                    last = nc.tensor.matmul(h_ps[i % 2][:], lhs[:, k, part], rhs[:, w, D:2 * D],
                                            start=(k == 0 and q == 0), stop=(k == KD - 1 and q == 2))
                if k == KD - 1 and q == 2:
                    last.then_inc(tile_mm, 1)

            def project(t, i, b):
                c = RING * t + i
                pe.wait_ge(tile_lo, c + 1)
                wait(pe, xf_ready, c - 1)
                for k in range(KD):
                    project_chunk(i, b, k)

            pe.wait_ge(tile_lo, 2)
            for k in range(KD):
                pe.wait_ge(wc0_hi, k + 1)
                for i in range(2):
                    project_chunk(i, 0, k, (0, 1))
                pe.wait_ge(wc0_ready, k + 1)
                for i in range(2):
                    project_chunk(i, 0, k, (2,))
            for i in range(2, RING):
                project(0, i, 0)
            with pe.Fori(1, ROUNDS // 2) as t:
                for i in range(RING):
                    project(t, i, 0)
            pe.wait_ge(wc1_ready, KD)
            with pe.Fori(ROUNDS // 2, ROUNDS - 1) as t:
                for i in range(RING):
                    project(t, i, 1)

            def transpose(s, kind, banks):
                per_bank, tok = kind
                if kind is WIDE:
                    pe.wait_ge(rows_in, DMA * (s + 1))
                else:
                    pe.wait_ge(rows_gathered, ME * DMA * (s - SHARED + 1))
                for f in banks:
                    pe.wait_ge(xt_lo, until(s, kind, KD, KD // 2) + f - 1)
                    for q in range(per_bank):
                        k = f * per_bank + q
                        for m in range(tok // P):
                            at = q * tok + m * P
                            last = nc.tensor.transpose(bank(s, f)[:, at:at + P], rows[:, m, k * P:(k + 1) * P], ident[:])
                    last.then_inc(xt_ps, 1)

            def hidden(s, ffn, j, kind):
                tok = kind[1]
                n = HC * s + j
                pe.wait_ge(w_ready, HALVES * ffn + 2 * j + 1)
                wait(pe, hf_ready, n - 1)
                if is_number(s, 0) and j < 2:
                    pe.wait_ge(xf_ready, NT - 1 + j)
                    pe.wait_ge(xt_lo, M)
                for k in range(KD):
                    if j == 0 and k % kind[0] == 0 and not is_number(s, 0):
                        pe.wait_ge(xt_lo, until(s, kind, KD, KD // 2) + k // kind[0] + 1)
                    part = slice(k * P, (k + 1) * P)
                    for q, (lhs, rhs) in enumerate(((w_hi, x_hi), (w_hi, x_lo), (w_lo, x_hi))):
                        last = nc.tensor.matmul(h_ps[j % 2][:, 0:tok], lhs[:, j, part], rhs[:, k, 0:tok],
                                                start=(k == 0 and q == 0), stop=(k == KD - 1 and q == 2))
                last.then_inc(h_mm, 1)

            def down(s, ffn, j, kind):
                groups = kind[1] // P
                n = HC * s + j
                pe.wait_ge(w_ready, HALVES * ffn + 2 * j + 2)
                pe.wait_ge(h_ready, n + 1)
                for m in range(groups):
                    if j == 0:
                        wait(pe, out_ready, until(s, kind, M, ME) - (groups - m - 1))
                    part = slice(m * P, (m + 1) * P)
                    for q, (lhs, rhs) in enumerate(((h_hi, w_hi), (h_hi, w_lo), (h_lo, w_hi))):
                        last = nc.tensor.matmul(y_ps[m][:], lhs[:, j % HB, part], rhs[:, j, D:2 * D],
                                                start=(j == 0 and q == 0), stop=(j == HC - 1 and q == 2))
                last.then_inc(y_mm, 1)

            def slot(s, ffn, nxt):
                kind = WIDE if ffn == 0 else NARROW
                for j in range(HC):
                    hidden(s, ffn, j, kind)
                    if j >= 2 and j < HC - 1:
                        down(s, ffn, j - 2, kind)
                    if isinstance(s, int) and s == 0 and j == 6:
                        pe.wait_ge(pick_ready, 1)
                        nc.tensor.matmul(t_ps[0][:, 0:NT], before[:], pick0[:], start=True, stop=True)
                        nc.tensor.matmul(t_ps[0][:, NT:2 * NT], ones[:], pick0[:], start=True, stop=True).then_inc(rank_ps, 1)
                banks = KD // nxt[0]
                transpose(s + 1, nxt, range(0, 2))
                down(s, ffn, HC - 3, kind)
                if banks > 2:
                    transpose(s + 1, nxt, range(2, banks))
                down(s, ffn, HC - 2, kind)
                down(s, ffn, HC - 1, kind)

            def short_slot(s):

                def hidden4(u):
                    if u < 2:
                        pe.wait_ge(hf_ready, HC * s - 1 + u)
                    else:
                        pe.wait_ge(flat_ready, u - 1)
                    if u == 0:
                        pe.wait_ge(xt_lo, until(s + 1, NARROW, KD, KD // 2))
                    for k in range(KD):
                        for q, (lhs, rhs) in enumerate(((x_hi, w_hi), (x_hi, w_lo), (x_lo, w_hi))):
                            last = nc.tensor.matmul(h_ps[u % 2][:], lhs[:, k, 0:P],
                                                    rhs[:, 4 * u:4 * u + 4, k * P:(k + 1) * P],
                                                    start=(k == 0 and q == 0), stop=(k == KD - 1 and q == 2))
                    last.then_inc(h_mm, 4)

                def back4(u):
                    pe.wait_ge(flat_ready, u + 1)
                    if u >= 2:
                        pe.wait_ge(hf_ready, HC * s + 4 * (u - 1))
                    for i in range(4):
                        part = slice(i * P, (i + 1) * P)
                        last = nc.tensor.transpose(t_ps[u % 2][:, part], hf[:, u % 2, part], ident[:])
                    last.then_inc(back_ps, 1)

                def down4(u):
                    pe.wait_ge(h_ready, HC * s + 4 * (u + 1))
                    if u == 0:
                        pe.wait_ge(out_ready, until(s, NARROW, M, ME))
                    for i in range(4):
                        j = 4 * u + i
                        part = slice(i * P, (i + 1) * P)
                        for q, (lhs, rhs) in enumerate(((h_hi, w_hi), (h_hi, w_lo), (h_lo, w_hi))):
                            last = nc.tensor.matmul(y_ps[0][:], lhs[:, u % HB, part], rhs[:, j, D:2 * D],
                                                    start=(j == 0 and q == 0), stop=(j == HC - 1 and q == 2))
                        last.then_inc(y_mm, 1)

                hidden4(0)
                hidden4(1)
                back4(0)
                for u in range(2, QUADS):
                    hidden4(u)
                    back4(u - 1)
                    down4(u - 2)
                back4(QUADS - 1)
                down4(QUADS - 2)
                pe.wait_ge(hf_ready, HC * (s + 1))
                transpose(s + 1, NARROW, range(0, 2))
                down4(QUADS - 1)

            pe.wait_ge(rows_in, DMA)
            for m in range(M):
                for k in range(KD):
                    last = nc.tensor.transpose(bank(0, m)[:, k * P:(k + 1) * P], rows[:, m, k * P:(k + 1) * P], ident[:])
                last.then_inc(xt_ps, 1)
            for i in range(RING):
                project(ROUNDS - 1, i, 1)
            slot(0, 0, WIDE)
            t0, end0, end1 = read_split(pe)
            with pe.Fori(1, SHARED - 1) as s:
                slot(s, 0, WIDE)
            slot(SHARED - 1, 0, NARROW)
            pe.wait_ge(acc_step, 2 + 2 * HC)
            pe.wait_ge(xt_lo, until(SHARED + 1, NARROW, KD, KD // 2))
            for e in range(2):
                last = nc.tensor.matmul(t_ps[e][:], ones[:], acc[:, e, :], start=True, stop=True)
            last.then_inc(bias_ps, 1)
            with pe.Fori(SHARED, end0) as s:
                slot(s, 1, NARROW)
            s1 = pe.snap(t0 + SHARED)
            with pe.If(end0 < s1):
                short_slot(end0)
            with pe.Fori(s1, end1) as s:
                slot(s, 2, NARROW)
            with pe.If(end1 < SLOTS):
                short_slot(end1)


def kernel(x, cond_1024, L0_cond_weight, L0_ffn_gate_w, L0_ffn_w1, L0_ffn_b1, L0_ffn_w2, L0_ffn_b2,
           L0_ffn_sw1, L0_ffn_sb1, L0_ffn_sw2, L0_ffn_sb2):
    import numpy as np
    import concourse.bacc as bacc
    from concourse.bass_utils import run_bass_kernel_spmd

    def lay(a):
        return np.ascontiguousarray(a)

    x, cond, w_cond, gate = (np.asarray(a) for a in (x, cond_1024, L0_cond_weight, L0_ffn_gate_w))
    w1, b1, w2, b2 = (np.asarray(a) for a in (L0_ffn_w1, L0_ffn_b1, L0_ffn_w2, L0_ffn_b2))
    sw1, sb1, sw2, sb2 = (np.asarray(a) for a in (L0_ffn_sw1, L0_ffn_sb1, L0_ffn_sw2, L0_ffn_sb2))
    rows = x.reshape(N, D)
    up = np.stack([sw1, w1[0], w1[1]]).reshape(3, KD, P, HC, P).transpose(0, 3, 2, 1, 4).reshape(3 * HC, P, D)
    down = np.stack([sw2, w2[0], w2[1]]).reshape(3 * HC, P, D)
    arrays = {
        "x_rows": lay(rows),
        "x_cols": lay(rows.reshape(NT, P, KD, P).transpose(0, 3, 2, 1).reshape(NT, P, D)),
        "cond": lay(cond.reshape(BATCHES, KD, P).transpose(2, 1, 0)),
        "w_cond": lay(w_cond.reshape(KD, P, D).transpose(1, 0, 2)),
        "w_pack": lay(np.stack([up, down], axis=1).reshape(3 * HALVES, P, D)),
        "b1_pack": lay(np.stack([sb1, b1[0], b1[1]]).reshape(3, HC, P).transpose(2, 0, 1)),
        "b2_rows": lay(np.stack([sb2, b2[0], b2[1]])),
        "gate": lay(gate),
    }
    nc = bacc.Bacc("TRN2", target_bir_lowering=False, num_devices=1)
    args = [nc.dram_tensor(n, a.shape, mybir.dt.from_np(a.dtype), kind="ExternalInput").ap() for n, a in arrays.items()]
    out = nc.dram_tensor("out", (N, D), F32, kind="ExternalOutput").ap()
    build(nc, *args, out)
    r = run_bass_kernel_spmd(nc, [arrays], core_ids=[0])
    return r.results[0]["out"].reshape(x.shape)
```
